# Optimizing a Trainium2 kernel written in Bass

```python
import numpy as np
import jax
import jax.numpy as jnp

def _softmax(x, axis=-1):
    return jax.nn.softmax(x, axis=axis)

def _gelu(x):
    return jax.nn.gelu(x, approximate=True)

def _silu(x):
    return jax.nn.silu(x)

def _sigmoid(x):
    return jax.nn.sigmoid(x)

def _layernorm(x, axis=-1, eps=1e-05):
    m = jnp.mean(x, axis=axis, keepdims=True)
    v = jnp.var(x, axis=axis, keepdims=True)
    return (x - m) / jnp.sqrt(v + eps)

def _scatter_add(tgt, idx, src, axis=0):
    return tgt.at[idx].add(src)

def _segment_sum(src, seg, n):
    return jax.ops.segment_sum(src, seg, n)
kernel_name = 'mk_conv_seq_d4_conv_nhwc512_r4_fe2bd6'

def setup_inputs(seed: int=0):
    np.random.seed(seed)
    _w = jnp.asarray

    def _rec_inputs():
        import jax
        import jax.numpy as jnp
        _gk = jax.random.key(seed)
        x = -0.0003929 + 0.9999 * jax.random.normal(jax.random.fold_in(_gk, 1), (8, 16, 16, 128), jnp.float32)
        return x
    x = _rec_inputs()

    def _L0_conv_setup():
        import jax, jax.numpy as jnp
        import numpy as np
        B, H, W, C = (8, 16, 16, 128)
        CQ = C // 8
        key = jax.random.key(seed)
        ks = jax.random.split(key, 7)
        s = 0.02
        return {'x': jax.random.normal(ks[0], (B, H, W, C), dtype=jnp.float32), 'Wq': jax.random.normal(ks[1], (C, CQ), dtype=jnp.float32) * s, 'bq': jnp.zeros((CQ,), dtype=jnp.float32), 'Wk': jax.random.normal(ks[2], (C, CQ), dtype=jnp.float32) * s, 'bk': jnp.zeros((CQ,), dtype=jnp.float32), 'Wv': jax.random.normal(ks[3], (C, C), dtype=jnp.float32) * s, 'bv': jnp.zeros((C,), dtype=jnp.float32), 'gamma': jnp.full((1,), 0.5, dtype=jnp.float32)}
    _L0_conv_all = _L0_conv_setup()
    _L0_conv_in = {k: v for k, v in _L0_conv_all.items() if k in ('Wq', 'bq', 'Wk', 'bk', 'Wv', 'bv', 'gamma')}
    del _L0_conv_all

    def _L1_conv_setup():
        import jax, jax.numpy as jnp
        import numpy as np
        SPARSITY = 0.01

        def _cas(n):
            t = jnp.arange(n, dtype=jnp.float32)
            a = 2.0 * jnp.pi * jnp.outer(t, t) / n
            return jnp.cos(a) + jnp.sin(a)

        def _dht2d(x):
            B, H, W, C = x.shape
            y = jnp.einsum('bhwc,cd->bhwd', x, _cas(C))
            return jnp.einsum('vw,bhwd->bhvd', _cas(W), y)
        key = jax.random.key(seed)
        k0, k1, k2, k3, k4 = jax.random.split(key, 5)
        B, H, W, C = (1, 45, 90, 128)
        nb, bs, f = (8, 16, 1)
        scale = 0.02
        x = jax.random.normal(k0, (B, H, W, C), jnp.float32)
        w1 = scale * jax.random.normal(k1, (2, nb, bs, bs * f), jnp.float32)
        b1 = scale * jax.random.normal(k2, (2, nb, bs * f), jnp.float32)
        w2 = scale * jax.random.normal(k3, (2, nb, bs * f, bs), jnp.float32)
        b2 = scale * jax.random.normal(k4, (2, nb, bs), jnp.float32)
        return {'x': x, 'w1': w1, 'b1': b1, 'w2': w2, 'b2': b2}
    _L1_conv_all = _L1_conv_setup()
    _L1_conv_in = {k: v for k, v in _L1_conv_all.items() if k in ('w1', 'b1', 'w2', 'b2')}
    del _L1_conv_all

    def _L2_conv_setup():
        import jax, jax.numpy as jnp
        import numpy as np
        B, H, W, C = (8, 16, 16, 128)
        CQ = C // 8
        key = jax.random.key(seed)
        ks = jax.random.split(key, 7)
        s = 0.02
        return {'x': jax.random.normal(ks[0], (B, H, W, C), dtype=jnp.float32), 'Wq': jax.random.normal(ks[1], (C, CQ), dtype=jnp.float32) * s, 'bq': jnp.zeros((CQ,), dtype=jnp.float32), 'Wk': jax.random.normal(ks[2], (C, CQ), dtype=jnp.float32) * s, 'bk': jnp.zeros((CQ,), dtype=jnp.float32), 'Wv': jax.random.normal(ks[3], (C, C), dtype=jnp.float32) * s, 'bv': jnp.zeros((C,), dtype=jnp.float32), 'gamma': jnp.full((1,), 0.5, dtype=jnp.float32)}
    _L2_conv_all = _L2_conv_setup()
    _L2_conv_in = {k: v for k, v in _L2_conv_all.items() if k in ('Wq', 'bq', 'Wk', 'bk', 'Wv', 'bv', 'gamma')}
    del _L2_conv_all

    def _L3_conv_setup():
        import jax, jax.numpy as jnp
        import numpy as np
        GROUPS = 32
        EPS = 1e-06
        key = jax.random.key(seed)
        ks = jax.random.split(key, 6)
        B, H, W, C = (4, 16, 16, 128)
        s = 1.0 / np.sqrt(C)
        return {'inputs': jax.random.normal(ks[0], (B, H, W, C), dtype=jnp.float32), 'gn_gamma': jnp.ones((C,), dtype=jnp.float32), 'gn_beta': jnp.zeros((C,), dtype=jnp.float32), 'wq': jax.random.normal(ks[1], (C, C), dtype=jnp.float32) * s, 'bq': jnp.zeros((C,), dtype=jnp.float32), 'wk': jax.random.normal(ks[2], (C, C), dtype=jnp.float32) * s, 'bk': jnp.zeros((C,), dtype=jnp.float32), 'wv': jax.random.normal(ks[3], (C, C), dtype=jnp.float32) * s, 'bv': jnp.zeros((C,), dtype=jnp.float32), 'wo': jax.random.normal(ks[4], (C, C), dtype=jnp.float32) * s, 'bo': jnp.zeros((C,), dtype=jnp.float32)}
    _L3_conv_all = _L3_conv_setup()
    _L3_conv_in = {k: v for k, v in _L3_conv_all.items() if k in ('gn_gamma', 'gn_beta', 'wq', 'bq', 'wk', 'bk', 'wv', 'bv', 'wo', 'bo')}
    del _L3_conv_all
    return {'x': x, 'L0_conv_Wq': _L0_conv_in['Wq'], 'L0_conv_bq': _L0_conv_in['bq'], 'L0_conv_Wk': _L0_conv_in['Wk'], 'L0_conv_bk': _L0_conv_in['bk'], 'L0_conv_Wv': _L0_conv_in['Wv'], 'L0_conv_bv': _L0_conv_in['bv'], 'L0_conv_gamma': _L0_conv_in['gamma'], 'L1_conv_w1': _L1_conv_in['w1'], 'L1_conv_b1': _L1_conv_in['b1'], 'L1_conv_w2': _L1_conv_in['w2'], 'L1_conv_b2': _L1_conv_in['b2'], 'L2_conv_Wq': _L2_conv_in['Wq'], 'L2_conv_bq': _L2_conv_in['bq'], 'L2_conv_Wk': _L2_conv_in['Wk'], 'L2_conv_bk': _L2_conv_in['bk'], 'L2_conv_Wv': _L2_conv_in['Wv'], 'L2_conv_bv': _L2_conv_in['bv'], 'L2_conv_gamma': _L2_conv_in['gamma'], 'L3_conv_gn_gamma': _L3_conv_in['gn_gamma'], 'L3_conv_gn_beta': _L3_conv_in['gn_beta'], 'L3_conv_wq': _L3_conv_in['wq'], 'L3_conv_bq': _L3_conv_in['bq'], 'L3_conv_wk': _L3_conv_in['wk'], 'L3_conv_bk': _L3_conv_in['bk'], 'L3_conv_wv': _L3_conv_in['wv'], 'L3_conv_bv': _L3_conv_in['bv'], 'L3_conv_wo': _L3_conv_in['wo'], 'L3_conv_bo': _L3_conv_in['bo']}

def reference(x, L0_conv_Wq, L0_conv_bq, L0_conv_Wk, L0_conv_bk, L0_conv_Wv, L0_conv_bv, L0_conv_gamma, L1_conv_w1, L1_conv_b1, L1_conv_w2, L1_conv_b2, L2_conv_Wq, L2_conv_bq, L2_conv_Wk, L2_conv_bk, L2_conv_Wv, L2_conv_bv, L2_conv_gamma, L3_conv_gn_gamma, L3_conv_gn_beta, L3_conv_wq, L3_conv_bq, L3_conv_wk, L3_conv_bk, L3_conv_wv, L3_conv_bv, L3_conv_wo, L3_conv_bo):
    import jax
    import jax.numpy as jnp

    def _L0_conv_ref(x, Wq, bq, Wk, bk, Wv, bv, gamma):
        import jax, jax.numpy as jnp
        import numpy as np
        B, H, W, C = (8, 16, 16, 128)
        CQ = C // 8
        b, h, w, c = x.shape
        hw = h * w
        q = (jnp.einsum('bhwc,cd->bhwd', x, Wq) + bq).reshape(b, hw, -1)
        k = (jnp.einsum('bhwc,cd->bhwd', x, Wk) + bk).reshape(b, hw, -1)
        energy = jnp.einsum('bnd,bmd->bnm', q, k)
        attn = jax.nn.softmax(energy, axis=-1)
        v = (jnp.einsum('bhwc,cd->bhwd', x, Wv) + bv).reshape(b, hw, c)
        out = jnp.einsum('bnm,bmc->bnc', attn, v).reshape(b, h, w, c)
        return gamma * out + x

    def _L1_conv_ref(x, w1, b1, w2, b2):
        import jax, jax.numpy as jnp
        import numpy as np
        SPARSITY = 0.01

        def _cas(n):
            t = jnp.arange(n, dtype=jnp.float32)
            a = 2.0 * jnp.pi * jnp.outer(t, t) / n
            return jnp.cos(a) + jnp.sin(a)

        def _dht2d(x):
            B, H, W, C = x.shape
            y = jnp.einsum('bhwc,cd->bhwd', x, _cas(C))
            return jnp.einsum('vw,bhwd->bhvd', _cas(W), y)
        bias = x
        B, H, W, C = x.shape
        nb, bs = (w1.shape[1], w1.shape[2])
        xh = _dht2d(x).reshape(B, H, W, nb, bs)
        xn = jnp.roll(jnp.flip(xh, axis=(1, 2)), shift=(1, 1), axis=(1, 2))
        w1a, w1b = (w1[0] + w1[1], w1[0] - w1[1])
        o1k = jax.nn.relu(0.5 * (jnp.einsum('bhwki,kio->bhwko', xh, w1a) + jnp.einsum('bhwki,kio->bhwko', xn, w1b)) + b1[0])
        o1n = jax.nn.relu(0.5 * (jnp.einsum('bhwki,kio->bhwko', xn, w1a) + jnp.einsum('bhwki,kio->bhwko', xh, w1b)) + b1[1])
        w2a, w2b = (w2[0] + w2[1], w2[0] - w2[1])
        o2k = 0.5 * (jnp.einsum('bhwki,kio->bhwko', o1k, w2a) + jnp.einsum('bhwki,kio->bhwko', o1n, w2b)) + b2[0]
        o2n = 0.5 * (jnp.einsum('bhwki,kio->bhwko', o1n, w2a) + jnp.einsum('bhwki,kio->bhwko', o2k, w2b)) + b2[1]
        y = (o2k + o2n).reshape(B, H, W, C)
        y = jnp.sign(y) * jax.nn.relu(jnp.abs(y) - SPARSITY)
        y = _dht2d(y) / (W * C)
        return y + bias

    def _L2_conv_ref(x, Wq, bq, Wk, bk, Wv, bv, gamma):
        import jax, jax.numpy as jnp
        import numpy as np
        B, H, W, C = (8, 16, 16, 128)
        CQ = C // 8
        b, h, w, c = x.shape
        hw = h * w
        q = (jnp.einsum('bhwc,cd->bhwd', x, Wq) + bq).reshape(b, hw, -1)
        k = (jnp.einsum('bhwc,cd->bhwd', x, Wk) + bk).reshape(b, hw, -1)
        energy = jnp.einsum('bnd,bmd->bnm', q, k)
        attn = jax.nn.softmax(energy, axis=-1)
        v = (jnp.einsum('bhwc,cd->bhwd', x, Wv) + bv).reshape(b, hw, c)
        out = jnp.einsum('bnm,bmc->bnc', attn, v).reshape(b, h, w, c)
        return gamma * out + x

    def _L3_conv_ref(inputs, gn_gamma, gn_beta, wq, bq, wk, bk, wv, bv, wo, bo):
        import jax, jax.numpy as jnp
        import numpy as np
        GROUPS = 32
        EPS = 1e-06
        B, H, W, C = inputs.shape
        xg = inputs.astype(jnp.float32).reshape(B, H, W, GROUPS, C // GROUPS)
        mean = jnp.mean(xg, axis=(1, 2, 4), keepdims=True)
        var = jnp.var(xg, axis=(1, 2, 4), keepdims=True)
        xg = (xg - mean) * jax.lax.rsqrt(var + EPS)
        x = xg.reshape(B, H, W, C) * gn_gamma + gn_beta
        q = jnp.einsum('bhwc,cd->bhwd', x, wq) + bq
        k = jnp.einsum('bhwc,cd->bhwd', x, wk) + bk
        v = jnp.einsum('bhwc,cd->bhwd', x, wv) + bv
        N = H * W
        q = q.reshape(B, N, C) * (1.0 / jnp.sqrt(jnp.float32(C)))
        k = k.reshape(B, N, C)
        v = v.reshape(B, N, C)
        scores = jnp.einsum('bnc,bmc->bnm', q, k)
        attn = jax.nn.softmax(scores.astype(jnp.float32), axis=-1).astype(q.dtype)
        out = jnp.einsum('bmc,bnm->bnc', v, attn)
        out = out.reshape(B, H, W, C)
        out = jnp.einsum('bhwc,cd->bhwd', out, wo) + bo
        return out + inputs

    def _gn(v, G=32, eps=1e-05):
        B_, H_, W_, C_ = v.shape
        g = v.reshape(B_, H_, W_, G, C_ // G)
        m = jnp.mean(g, axis=(1, 2, 4), keepdims=True)
        s = jnp.var(g, axis=(1, 2, 4), keepdims=True)
        return ((g - m) / jnp.sqrt(s + eps)).reshape(v.shape)

    def _ln_c(v, eps=1e-06):
        m = jnp.mean(v, axis=-1, keepdims=True)
        s = jnp.var(v, axis=-1, keepdims=True)
        return (v - m) / jnp.sqrt(s + eps)

    def _ln_t(v, eps=1e-05):
        m = jnp.mean(v, axis=-1, keepdims=True)
        s = jnp.var(v, axis=-1, keepdims=True)
        return (v - m) / jnp.sqrt(s + eps)

    def _to_tokens(v):
        B_, H_, W_, C_ = v.shape
        return v.reshape(B_, H_ * W_, C_)

    def _from_tokens(t, like):
        return t.reshape(like.shape)
    x = _L0_conv_ref(x, L0_conv_Wq, L0_conv_bq, L0_conv_Wk, L0_conv_bk, L0_conv_Wv, L0_conv_bv, L0_conv_gamma)
    x = _L1_conv_ref(x, L1_conv_w1, L1_conv_b1, L1_conv_w2, L1_conv_b2)
    x = _L2_conv_ref(x, L2_conv_Wq, L2_conv_bq, L2_conv_Wk, L2_conv_bk, L2_conv_Wv, L2_conv_bv, L2_conv_gamma)
    x = _L3_conv_ref(x, L3_conv_gn_gamma, L3_conv_gn_beta, L3_conv_wq, L3_conv_bq, L3_conv_wk, L3_conv_bk, L3_conv_wv, L3_conv_bv, L3_conv_wo, L3_conv_bo)
    return x

_drawn_inputs = setup_inputs


def setup_inputs(seed=0):
    import zlib

    import numpy as np

    out = dict(_drawn_inputs(seed))
    spreads = {'L0_conv_bq': (0.0, 0.8),
     'L0_conv_bk': (0.0, 2.0),
     'L0_conv_bv': (0.0, 0.1),
     'L2_conv_bq': (0.0, 0.8),
     'L2_conv_bk': (0.0, 2.0),
     'L2_conv_bv': (0.0, 0.1),
     'L3_conv_gn_gamma': (1.0, 0.2),
     'L3_conv_gn_beta': (0.0, 0.1),
     'L3_conv_bq': (0.0, 0.624),
     'L3_conv_bk': (0.0, 2.0),
     'L3_conv_bv': (0.0, 0.1),
     'L3_conv_bo': (0.0, 0.1)}
    factors = {'L0_conv_Wq': 8.0,
     'L0_conv_Wk': 8.0,
     'L0_conv_Wv': 5.757,
     'L1_conv_w1': 8.0,
     'L1_conv_b1': 64.0,
     'L1_conv_w2': 8.0,
     'L1_conv_b2': 31.682,
     'L2_conv_Wq': 8.0,
     'L2_conv_Wk': 8.0,
     'L2_conv_Wv': 4.701}
    for name, (base, spread) in spreads.items():
        noise = np.random.default_rng([zlib.crc32(name.encode()), seed]).standard_normal(out[name].shape)
        drawn = base * np.exp(spread * noise) if base else spread * noise
        out[name] = jnp.asarray(drawn.astype(out[name].dtype))
    for name, factor in factors.items():
        out[name] = (out[name] * factor).astype(out[name].dtype)
    return out
```

```python
from contextlib import ExitStack

import numpy as np

import concourse.bass as bass
from concourse import mybir

BATCH, HEIGHT, WIDTH, C = 8, 16, 16, 128
TOKENS = HEIGHT * WIDTH
TILE = 128
TILES = TOKENS // TILE
IMAGES = 2
PAIRS = BATCH // IMAGES
PT = IMAGES * TILES
CQ = C // 8
CV = C + 1
BLOCKS, BS = 8, 16
GROUPS = 32
SHRINK = 0.01
EPS = 1e-6
SCALE3 = 1.0 / float(np.sqrt(np.float32(C)))
FMAX = 3.0e38

ROW_RUNS = [[(0, 4), (8, 1), (13, 3)], [(4, 4), (9, 4)]]
ROWS = [[h + k for h, n in runs for k in range(n)] for runs in ROW_RUNS]
DMAS = sum(len(runs) for runs in ROW_RUNS)

FIXED = 4
HALF0 = TILE // 2 + FIXED // 2
HALF1 = TILE // 2
WIDE0 = 2 * HALF0
FREQ = WIDE0 + TILE


def frequency_orders():
    forward, backward = [], []
    for rows in ROWS:
        fixed, first, second = [], [], []
        for h in rows:
            for v in range(WIDTH):
                partner = (-h % HEIGHT, -v % WIDTH)
                if partner == (h, v):
                    fixed.append((h, v))
                elif partner not in first:
                    first.append((h, v))
                    second.append(partner)
        f = len(fixed) // 2
        a = fixed[:f] + first + fixed[f:]
        b = fixed[:f] + second + fixed[f:]
        forward.append(a + b)
        backward.append(a[:TILE // 2] + b[f:])
    return forward, backward


def shape_constants():
    def cas(a, n):
        t = 2.0 * np.pi * ((a % n) / n)
        return np.cos(t) + np.sin(t)

    c = np.arange(C)
    eye = np.eye(C)
    forward_order, backward_order = frequency_orders()
    forward, backward = [], []
    for rows, fo, bo in zip(ROWS, forward_order, backward_order):
        tokens = [(h, w) for h in rows for w in range(WIDTH)]
        def table(order):
            return np.array([[cas(w * v, WIDTH) if h == g else 0.0 for g, v in order]
                             for h, w in tokens])
        forward.append(table(fo))
        backward.append(table(bo).T / (WIDTH * C))
    mask = np.kron(np.eye(BLOCKS), np.ones((BS, BS)))
    size = C // GROUPS
    half_average = np.kron(np.eye(GROUPS), np.full((size, size), 0.5 / size))
    return {
        "ident": eye, "cas": cas(np.outer(c, c), C), "forward": np.hstack(forward),
        "backward": np.hstack(backward), "mask": mask, "half_average": half_average,
        "minus_half_average": -half_average, "deviation": eye - half_average,
    }


CONSTANTS = ["cas", "forward", "backward", "mask", "half_average", "minus_half_average",
             "deviation"]
CONSTANT_WIDTHS = [C, FREQ, TILES * TILE, C, C, C, C]
SMALL_WIDTH = 4 * C + 2 * (C + 1)
COLUMNS = ["b1k", "b1n", "b2k", "b2n", "gn_gamma", "gn_beta", "bq3", "bk3", "bv3",
           "gamma0", "gamma2"]


def build(nc, x, ident_d, constants_d, small_d, values_d, blocks_d, columns_d, layer3_d, out):
    fp32 = mybir.dt.float32
    ALU = mybir.AluOpType
    ACT = mybir.ActivationFunctionType

    ctx = ExitStack()
    with ctx:
        def sb(name, shape):
            return ctx.enter_context(nc.sbuf_tensor(name, shape, fp32))

        def sem(name):
            return ctx.enter_context(nc.semaphore(name))

        ident = sb("ident", [C, C])
        constants = sb("constants", [C, sum(CONSTANT_WIDTHS)])
        at, views = 0, {}
        for name, width in zip(CONSTANTS, CONSTANT_WIDTHS):
            views[name] = constants[:, at:at + width]
            at += width
        small = sb("small", [CQ, SMALL_WIDTH])
        values = sb("values", [C, 5 * C])
        blocks = sb("blocks", [C, 2, 3, BS])
        columns = sb("columns", [C, len(COLUMNS)])
        column = {n: columns[:, k:k + 1] for k, n in enumerate(COLUMNS)}
        layer3 = sb("layer3", [C, 4 * C])

        uw = {n: sb(f"uw{n}", [C, C + 1]) for n in (0, 2, 3)}
        vw = {n: sb(f"vw{n}", [C, CV]) for n in (0, 2, 3)}
        vb = {n: sb(f"vb{n}", [C, CV]) for n in (0, 2, 3)}
        bq3_rows = sb("bq3_rows", [C, C])
        bv3_rows = sb("bv3_rows", [C, C])
        half_sum = sb("half_sum", [C, 2, 3, BS])
        sum_dif = sb("sum_dif", [C, 2, 3, BS])
        diagonal = sb("diagonal", [C, 2, 3, C])
        i_plus_b = sb("i_plus_b", [C, C])
        mixer = sb("mixer", [C, 4, C])
        y_bias = sb("y_bias", [C, 2])
        minus_half = sb("minus_half", [C, IMAGES])

        x_in = sb("x_in", [TILE, PT, C])
        x1 = sb("x1", [TILE, PT, C])
        x2 = sb("x2", [TILE, PT, C])
        x3 = sb("x3", [TILE, PT, C])
        x_out = sb("x_out", [TILE, PT, C])
        xt = {n: sb(f"xt{n}", [C, PT, TILE]) for n in (0, 2, 3)}
        u = {n: sb(f"u{n}", [C, PT, TILE]) for n in (0, 2, 3)}
        v = {n: sb(f"v{n}", [TILE, PT, CV]) for n in (0, 2, 3)}
        negated = {n: sb(f"negated{n}", [TILE, PT, TOKENS]) for n in (0, 2, 3)}
        lowest = {n: sb(f"lowest{n}", [TILE, PT]) for n in (0, 2, 3)}
        probs = {n: sb(f"probs{n}", [TILE, PT, TOKENS]) for n in (0, 2, 3)}
        total = {n: sb(f"total{n}", [TILE, PT]) for n in (0, 2, 3)}
        inverse = {n: sb(f"inverse{n}", [TILE, PT]) for n in (0, 2, 3)}
        probs_t = {n: sb(f"probs_t{n}", [TILE, IMAGES, TILES, TOKENS]) for n in (0, 2, 3)}
        z = sb("z", [C, IMAGES, FREQ])
        k_act = sb("k_act", [C, IMAGES, FREQ])
        n_act = sb("n_act", [C, IMAGES, FREQ])
        y_top = sb("y_top", [C, PT, TILE])
        y = sb("y", [C, PT, TILE])
        g = sb("g", [TILE, PT, C])
        stats = sb("stats", [C, IMAGES, 2, 3])
        square = sb("square", [C, IMAGES, 2])
        spread = sb("spread", [C, IMAGES, 2])
        group_mean = sb("group_mean", [C, IMAGES])
        group_var = sb("group_var", [C, IMAGES])
        rstd = sb("rstd", [C, IMAGES])
        gn_scale = sb("gn_scale", [C, IMAGES])
        gn_product = sb("gn_product", [C, IMAGES])
        gn_shift = sb("gn_shift", [C, IMAGES])

        banks = ctx.enter_context(nc.psum_tensor("banks", [128, 8, 512], fp32))
        first_bank = {0: 0, 1: 0, 2: 4, 3: 4}

        def bank(layer, k):
            return banks[:, first_bank[layer] + k, :]

        def two_banks(layer, k, width):
            at = first_bank[layer] + k
            return banks[:, at:at + 2, 0:width]

        ident_loaded = sem("ident_loaded")
        small_loaded = sem("small_loaded")
        values_loaded = sem("values_loaded")
        columns_loaded = sem("columns_loaded")
        blocks_loaded = sem("blocks_loaded")
        constants_loaded = sem("constants_loaded")
        uw_psum = {n: sem(f"uw_psum{n}") for n in (0, 2, 3)}
        weights_ready = {n: sem(f"weights_ready{n}") for n in (0, 2, 3)}
        rows3_ready = sem("rows3_ready")
        halves_made = sem("halves_made")
        diagonal_ready = sem("diagonal_ready")
        mixer_psum = sem("mixer_psum")
        mixer_ready = sem("mixer_ready")
        minus_half_ready = sem("minus_half_ready")

        x_loaded = sem("x_loaded")
        back_dmas = sem("back_dmas")
        xt_psum = {n: sem(f"xt_psum{n}") for n in (0, 2, 3)}
        xt_ready = {n: sem(f"xt_ready{n}") for n in (0, 2)}
        u_psum = {n: sem(f"u_psum{n}") for n in (0, 2, 3)}
        u_ready = {n: sem(f"u_ready{n}") for n in (0, 2, 3)}
        v_psum = {n: sem(f"v_psum{n}") for n in (0, 2, 3)}
        v_ready = {n: sem(f"v_ready{n}") for n in (0, 2, 3)}
        energy_psum = {n: sem(f"energy_psum{n}") for n in (0, 2, 3)}
        negated_ready = {n: sem(f"negated_ready{n}") for n in (0, 2, 3)}
        probs_ready = {n: sem(f"probs_ready{n}") for n in (0, 2, 3)}
        probs_t_psum = {n: sem(f"probs_t_psum{n}") for n in (0, 2, 3)}
        probs_t_ready_a = {n: sem(f"probs_t_ready_a{n}") for n in (0, 2, 3)}
        probs_t_ready_b = {n: sem(f"probs_t_ready_b{n}") for n in (0, 2, 3)}
        inverse_ready = {n: sem(f"inverse_ready{n}") for n in (0, 2, 3)}
        mixed_psum = {n: sem(f"mixed_psum{n}") for n in (0, 2, 3)}
        attended = {n: sem(f"attended{n}") for n in (0, 2, 3)}

        z_psum, z_ready = sem("z_psum"), sem("z_ready")
        w_psum = sem("w_psum")
        act_ready_a, act_ready_b = sem("act_ready_a"), sem("act_ready_b")
        y_psum, y_top_ready, y_ready = sem("y_psum"), sem("y_top_ready"), sem("y_ready")
        g_psum, g_ready = sem("g_psum"), sem("g_ready")
        back_psum, x2_ready = sem("back_psum"), sem("x2_ready")

        stats_ready = sem("stats_ready")
        deviation_psum, square_ready = sem("deviation_psum"), sem("square_ready")
        group_mean_ready, spread_ready = sem("group_mean_ready"), sem("spread_ready")
        variance_psum, group_var_ready = sem("variance_psum"), sem("group_var_ready")
        rstd_ready, gn_scale_ready = sem("rstd_ready"), sem("gn_scale_ready")
        gn_product_ready, gn_shift_ready = sem("gn_product_ready"), sem("gn_shift_ready")
        normed_ready_a, normed_ready_b = sem("normed_ready_a"), sem("normed_ready_b")

        x_of = {0: x_in, 2: x2, 3: x3}
        to = {0: x1, 2: x3, 3: x_out}
        weights_parts = {0: 5, 2: 5, 3: 4}

        def partners(t, image, start, step, length):
            whole = t[:, image, start:start + 1]
            return bass.AP(t, whole.offset, [list(whole.ap[0]), [step, 2], [1, length]])

        def halves(flat):
            return flat.rearrange("p (a b) -> p a b", a=2)

        x_pairs = x.rearrange("(i b) h w c -> i (h w) b c", b=IMAGES)
        out_pairs = out.rearrange("(i b) h w c -> i (h w) b c", b=IMAGES)

        def pieces():
            for tile, runs in enumerate(ROW_RUNS):
                p = 0
                for h, n in runs:
                    yield tile, p, h * WIDTH, n * WIDTH
                    p += n * WIDTH

        block = ctx.enter_context(nc.Block())

        @block.sync
        def _(sp):
            def load(i):
                if not (isinstance(i, int) and i == 0):
                    sp.wait_ge(attended[0], i * IMAGES)
                for tile, p, token, n in pieces():
                    sp.dma_start(x_in[p:p + n, tile::TILES, :],
                                 x_pairs[i, token:token + n]).then_inc(x_loaded, 16)

            def store(i):
                sp.wait_ge(attended[3], i * IMAGES + IMAGES + 1)
                for tile, p, token, n in pieces():
                    sp.dma_start(out_pairs[i, token:token + n],
                                 x_out[p:p + n, tile::TILES, :]).then_inc(back_dmas, 16)

            load(0)
            sp.dma_start(values[:, :], values_d).then_inc(values_loaded, 16)
            sp.dma_start(blocks[:, :, :, :], blocks_d).then_inc(blocks_loaded, 16)
            sp.dma_start(layer3[:, :], layer3_d).then_inc(back_dmas, 16)
            load(1)
            with sp.Fori(0, PAIRS - 2) as j:
                load(j + 2)
                store(j)
            for i in range(PAIRS - 2, PAIRS):
                store(i)
            sp.wait_ge(back_dmas, 16 + PAIRS * DMAS * 16)

        @block.gpsimd
        def _(pool):
            pool.memset(minus_half[:, :], -0.5).then_inc(minus_half_ready, 1)
            pool.wait_ge(blocks_loaded, 16)
            pool.tensor_tensor(sum_dif[:, 0], blocks[:, 0], blocks[:, 1],
                               ALU.add).then_inc(halves_made, 1)
            pool.tensor_tensor(sum_dif[:, 1], blocks[:, 0], blocks[:, 1],
                               ALU.subtract).then_inc(halves_made, 1)
            pool.wait_ge(halves_made, 2)
            pool.tensor_scalar(half_sum[:, :, :, :], sum_dif[:, :, :, :], 0.5, None,
                               ALU.mult).then_inc(halves_made, 1)
            pool.wait_ge(halves_made, 3)
            pool.wait_ge(constants_loaded, 16)
            mask = views["mask"].rearrange("p (k o) -> p k o", k=BLOCKS)
            for part in range(2):
                for which in range(3):
                    pool.tensor_tensor(
                        diagonal[:, part, which].rearrange("p (k o) -> p k o", k=BLOCKS), mask,
                        half_sum[:, part, which].unsqueeze(1).to_broadcast([C, BLOCKS, BS]),
                        ALU.mult).then_inc(diagonal_ready, 1)
            pool.wait_ge(diagonal_ready, 6)
            pool.wait_ge(ident_loaded, 16)
            pool.tensor_tensor(i_plus_b[:, :], diagonal[:, 1, 1], ident[:, :],
                               ALU.add).then_inc(diagonal_ready, 1)
            pool.wait_ge(columns_loaded, 16)
            for rows, name in ((bq3_rows, "bq3"), (bv3_rows, "bv3")):
                pool.tensor_copy(rows[:, :], column[name].to_broadcast([C, C])).then_inc(
                    rows3_ready, 1)
            pool.wait_ge(minus_half_ready, 1)
            with pool.Fori(0, PAIRS) as i:
                pool.wait_ge(group_var_ready, i + 1)
                pool.tensor_tensor(rstd[:, :], group_var[:, :], minus_half[:, :],
                                   ALU.pow).then_inc(rstd_ready, 1)

        @block.tensor
        def _(pe):
            def small_products(n, base):
                b = bank(2, 0 if n == 0 else 1 if n == 2 else 2)
                if n == 3:
                    wq_t, wk_t = layer3[:, 0:C], layer3[:, C:2 * C]
                    bq, bk, bq_rows = column["bq3"], column["bk3"], bq3_rows[:, :]
                else:
                    wq_t, wk_t = small[:, base:base + C], small[:, base + C:base + 2 * C]
                    bq_rows = small[:, base + 2 * C:base + 3 * C]
                    bq, bk = bq_rows[:, 0:1], small[:, base + 3 * C:base + 3 * C + 1]
                nc.tensor.matmul(b[:, 0:C], wq_t, wk_t, start=True, stop=True)
                nc.tensor.matmul(b[:, C:C + 1], wk_t, bq, start=True, stop=True)
                nc.tensor.matmul(b[:, C + 1:C + 2], wq_t, bk, start=True, stop=True)
                return nc.tensor.matmul(b[:, C + 2:C + 3], bq_rows, bk, start=True, stop=True)

            def setup_02():
                pe.wait_ge(small_loaded, 16)
                small_products(0, 0).then_inc(uw_psum[0], 1)
                small_products(2, 3 * C + 1).then_inc(uw_psum[2], 1)

            def setup_3():
                pe.wait_ge(back_dmas, 16)
                pe.wait_ge(columns_loaded, 16)
                pe.wait_ge(rows3_ready, 2)
                small_products(3, 0)
                wv_t, wo = layer3[:, 2 * C:3 * C], layer3[:, 3 * C:4 * C]
                nc.tensor.matmul(bank(2, 3)[:, 0:C], wv_t, wo, start=True, stop=True)
                nc.tensor.matmul(bank(2, 3)[:, C:2 * C], bv3_rows[:, :], wo,
                                 start=True, stop=True).then_inc(uw_psum[3], 1)

            def setup_1():
                pe.wait_ge(diagonal_ready, 7)
                pe.wait_ge(weights_ready[0], weights_parts[0])
                pe.wait_ge(weights_ready[2], weights_parts[2])
                b = bank(2, 0)
                cas = views["cas"]
                a2, a2_t, b2_t = diagonal[:, 0, 1], diagonal[:, 0, 2], diagonal[:, 1, 2]
                nc.tensor.matmul(b[:, 0:C], cas, diagonal[:, 0, 0], start=True, stop=True)
                nc.tensor.matmul(b[:, C:2 * C], cas, diagonal[:, 1, 0], start=True, stop=True)
                nc.tensor.matmul(b[:, 2 * C:3 * C], a2_t, i_plus_b[:, :], start=True, stop=True)
                nc.tensor.matmul(b[:, 3 * C:4 * C], b2_t, i_plus_b[:, :], start=True, stop=False)
                nc.tensor.matmul(b[:, 3 * C:4 * C], ident[:, :], a2, start=False, stop=True)
                nc.tensor.matmul(bank(2, 1)[:, 0:1], i_plus_b[:, :], column["b2k"],
                                 start=True, stop=True).then_inc(mixer_psum, 1)

            def transpose_x(n, i):
                if n == 0:
                    pe.wait_ge(x_loaded, (i + 1) * (DMAS * 16))
                elif n == 2:
                    pe.wait_ge(x2_ready, i + 1)
                    pe.wait_ge(attended[3], i * IMAGES + 1)
                else:
                    pe.wait_ge(attended[2], i * IMAGES + IMAGES)
                for t in range(PT):
                    mm = nc.tensor.transpose(
                        bank(n, t // TILES)[:, t % TILES * TILE:(t % TILES + 1) * TILE],
                        x_of[n][:, t, :], ident[:, :])
                mm.then_inc(xt_psum[n], 1)

            def project_u(n, i):
                if n == 3:
                    pe.wait_ge(normed_ready_a, i + 1)
                    pe.wait_ge(normed_ready_b, i + 1)
                else:
                    pe.wait_ge(xt_ready[n], i + 1)
                if n == 0 and not (isinstance(i, int) and i == 0):
                    pe.wait_ge(x2_ready, i)
                nc.tensor.matmul(bank(n, 3), uw[n][:, 0:C], xt[n][:, :, :],
                                 start=True, stop=True).then_inc(u_psum[n], 1)

            def project_v(n, i):
                for t in range(PT):
                    at = t % TILES * CV
                    mm = nc.tensor.matmul(bank(n, 1 + t // TILES)[:, at:at + CV],
                                          xt[n][:, t, :], vw[n][:, :], start=True, stop=True)
                mm.then_inc(v_psum[n], 1)

            def energies(n, i):
                pe.wait_ge(u_ready[n], i + 1)
                for image in range(IMAGES):
                    for tile in range(TILES):
                        t = image * TILES + tile
                        mm = nc.tensor.matmul(
                            bank(n, 3 * image)[:, tile * TOKENS:(tile + 1) * TOKENS],
                            u[n][:, t, :], xt[n][:, image * TILES:(image + 1) * TILES, :],
                            start=True, stop=True)
                    mm.then_inc(energy_psum[n], 1)

            def transpose_probs(n, i):
                pe.wait_ge(v_ready[n], i + 1)
                for image in range(IMAGES):
                    pe.wait_ge(probs_ready[n], i * PT + (image + 1) * TILES)
                    for m in range(TILES):
                        for tile in range(TILES):
                            at = m * TOKENS + tile * TILE
                            mm = nc.tensor.transpose(
                                bank(n, 1 + image)[:, at:at + TILE],
                                probs[n][:, image * TILES + tile, m * TILE:(m + 1) * TILE],
                                ident[:, :])
                    mm.then_inc(probs_t_psum[n], 1)

            def mix_values(n, i):
                for image in range(IMAGES):
                    pe.wait_ge((probs_t_ready_a, probs_t_ready_b)[image][n], i + 1)
                    for tile in range(TILES):
                        for m in range(TILES):
                            mm = nc.tensor.matmul(
                                bank(n, 3 * image)[:, tile * C:(tile + 1) * C],
                                probs_t[n][:, image, m, tile * TILE:(tile + 1) * TILE],
                                v[n][:, image * TILES + m, 0:C],
                                start=(m == 0), stop=(m == TILES - 1))
                    mm.then_inc(mixed_psum[n], 1)

            def forward_tokens(i):
                for image in range(IMAGES):
                    pe.wait_ge(attended[0], i * IMAGES + image + 1)
                    b = bank(1, 1 + image)
                    nc.tensor.matmul(b[:, 0:WIDE0], x1[:, image * TILES, :],
                                     views["forward"][:, 0:WIDE0], start=True, stop=True)
                    mm = nc.tensor.matmul(b[:, WIDE0:FREQ], x1[:, image * TILES + 1, :],
                                          views["forward"][:, WIDE0:FREQ], start=True, stop=True)
                mm.then_inc(z_psum, 1)

            def first_product(i):
                pe.wait_ge(z_ready, i + 1)
                for image in range(IMAGES):
                    b = bank(1, 3 * image)
                    nc.tensor.matmul(b[:, 0:FREQ], mixer[:, 0], z[:, image, :],
                                     start=True, stop=False)
                    nc.tensor.matmul(halves(b[:, 0:WIDE0]), mixer[:, 1],
                                     partners(z, image, HALF0, -HALF0, HALF0),
                                     start=False, stop=False)
                    nc.tensor.matmul(halves(b[:, WIDE0:FREQ]), mixer[:, 1],
                                     partners(z, image, WIDE0 + HALF1, -HALF1, HALF1),
                                     start=False, stop=True).then_inc(w_psum, 1)

            def second_product(i):
                b = bank(1, 1)
                skip = HALF0 + FIXED // 2
                for image in range(IMAGES):
                    pe.wait_ge((act_ready_a, act_ready_b)[image], i + 1)
                    at = image * TOKENS
                    own = [partners(k_act, image, 0, skip, TILE // 2),
                           partners(k_act, image, WIDE0, HALF1, HALF1)]
                    other = [partners(n_act, image, HALF0, FIXED // 2 - HALF0, TILE // 2),
                             partners(n_act, image, WIDE0 + HALF1, -HALF1, HALF1)]
                    for tile in range(TILES):
                        o = halves(b[:, at + tile * TILE:at + (tile + 1) * TILE])
                        nc.tensor.matmul(o, mixer[:, 2], own[tile], start=True, stop=False)
                        mm = nc.tensor.matmul(o, mixer[:, 3], other[tile], start=False, stop=True)
                mm.then_inc(y_psum, 1)

            def backward_channels(i):
                pe.wait_ge(y_ready, i + 1)
                for t in range(PT):
                    mm = nc.tensor.matmul(bank(1, 2)[:, t * C:(t + 1) * C], y[:, t, :],
                                          views["cas"], start=True, stop=True)
                mm.then_inc(g_psum, 1)

            def backward_tokens(i):
                pe.wait_ge(g_ready, i + 1)
                for t in range(PT):
                    tile = t % TILES
                    mm = nc.tensor.matmul(
                        bank(1, 3)[:, t * C:(t + 1) * C],
                        views["backward"][:, tile * TILE:(tile + 1) * TILE], g[:, t, :],
                        start=True, stop=True)
                mm.then_inc(back_psum, 1)

            def group_deviations(i):
                pe.wait_ge(stats_ready, i + 1)
                b = bank(3, 3)[:, 0:2 * IMAGES].rearrange("p (a e) -> p a e", a=IMAGES)
                means = stats[:, :, :, 1]
                others = bass.AP(stats, stats[:, :, 1, 1].offset,
                                 [list(means.ap[0]), list(means.ap[1]), [-means.ap[2][0], 2]])
                nc.tensor.matmul(b, views["deviation"], means, start=True, stop=False)
                nc.tensor.matmul(b, views["minus_half_average"], others,
                                 start=False, stop=True).then_inc(deviation_psum, 1)

            def group_variances(i):
                pe.wait_ge(spread_ready, i + 1)
                nc.tensor.matmul(bank(3, 2)[:, 0:IMAGES], views["half_average"],
                                 spread[:, :, 0], start=True, stop=False)
                nc.tensor.matmul(bank(3, 2)[:, 0:IMAGES], views["half_average"],
                                 spread[:, :, 1], start=False, stop=True).then_inc(
                                     variance_psum, 1)

            pe.wait_ge(ident_loaded, 16)
            setup_02()
            transpose_x(0, 0)
            pe.wait_ge(weights_ready[0], weights_parts[0])
            project_u(0, 0)
            project_v(0, 0)
            energies(0, 0)
            setup_1()
            transpose_probs(0, 0)
            setup_3()
            mix_values(0, 0)
            forward_tokens(0)
            pe.wait_ge(mixer_ready, 3)
            first_product(0)
            second_product(0)
            backward_channels(0)
            backward_tokens(0)
            pe.wait_ge(weights_ready[3], weights_parts[3])
            pe.wait_ge(attended[3], 1)

            with pe.Fori(0, PAIRS - 1) as j:
                i = j + 1
                transpose_x(0, i)
                transpose_x(2, j)
                project_u(0, i)
                project_v(0, i)
                project_u(2, j)
                project_v(2, j)
                energies(0, i)
                energies(2, j)
                transpose_probs(0, i)
                transpose_probs(2, j)
                mix_values(0, i)
                mix_values(2, j)
                forward_tokens(i)
                transpose_x(3, j)
                first_product(i)
                group_deviations(j)
                second_product(i)
                group_variances(j)
                backward_channels(i)
                project_u(3, j)
                project_v(3, j)
                energies(3, j)
                backward_tokens(i)
                transpose_probs(3, j)
                mix_values(3, j)

            i = PAIRS - 1
            transpose_x(2, i)
            project_u(2, i)
            project_v(2, i)
            energies(2, i)
            transpose_probs(2, i)
            mix_values(2, i)
            transpose_x(3, i)
            group_deviations(i)
            group_variances(i)
            project_u(3, i)
            project_v(3, i)
            energies(3, i)
            transpose_probs(3, i)
            mix_values(3, i)

        @block.scalar
        def _(act):
            def move_xt(n, i):
                act.wait_ge(xt_psum[n], i + 1)
                nc.scalar.activation(xt[n][:, :, :].rearrange("p (a t) k -> p a (t k)", a=IMAGES),
                                     two_banks(n, 0, TOKENS), ACT.Copy).then_inc(xt_ready[n], 1)

            def move_u(n, i):
                act.wait_ge(u_psum[n], i + 1)
                nc.scalar.activation(u[n][:, :, :].rearrange("p t k -> p (t k)"), bank(n, 3),
                                     ACT.Identity, bias=uw[n][:, C:C + 1]).then_inc(u_ready[n], 1)

            def exponents(n, i):
                for t in range(PT):
                    act.wait_ge(negated_ready[n], i * PT + t + 1)
                    nc.scalar.activation(probs[n][:, t, :], negated[n][:, t, :], ACT.Exp,
                                         bias=lowest[n][:, t:t + 1], scale=-1.0,
                                         accum_out=total[n][:, t:t + 1]).then_inc(
                                             probs_ready[n], 1)

            def move_probs_a(n, i):
                act.wait_ge(probs_t_psum[n], i * IMAGES + 1)
                nc.scalar.activation(probs_t[n][:, 0].rearrange("p m k -> p (m k)"), bank(n, 1),
                                     ACT.Copy).then_inc(probs_t_ready_a[n], 1)

            def move_z(i):
                act.wait_ge(z_psum, i + 1)
                nc.scalar.activation(z[:, :, :], two_banks(1, 1, FREQ), ACT.Copy).then_inc(
                    z_ready, 1)

            def activate_a(i):
                act.wait_ge(w_psum, i * IMAGES + 1)
                b = bank(1, 0)[:, 0:FREQ]
                nc.scalar.activation(k_act[:, 0, :], b, ACT.Relu, bias=column["b1k"])
                nc.scalar.activation(n_act[:, 0, :], b, ACT.Relu, bias=column["b1n"]).then_inc(
                    act_ready_a, 1)

            def shrink_top(i):
                act.wait_ge(y_psum, i + 1)
                nc.scalar.activation(y_top[:, :, :].rearrange("p t k -> p (t k)"), bank(1, 1),
                                     ACT.Relu, bias=y_bias[:, 0:1]).then_inc(y_top_ready, 1)

            def move_g(i):
                act.wait_ge(g_psum, i + 1)
                nc.scalar.activation(g[:, :, :].rearrange("p t k -> p (t k)"), bank(1, 2),
                                     ACT.Copy).then_inc(g_ready, 1)

            def square_deviations(i):
                act.wait_ge(deviation_psum, i + 1)
                nc.scalar.activation(square[:, :, :].rearrange("p a e -> p (a e)"),
                                     bank(3, 3)[:, 0:2 * IMAGES], ACT.Square).then_inc(square_ready, 1)

            def normalize_a(i):
                act.wait_ge(gn_shift_ready, i + 1)
                nc.scalar.activation(xt[3][:, 0:TILES, :].rearrange("p t k -> p (t k)"),
                                     bank(3, 0)[:, 0:TOKENS], ACT.Identity,
                                     bias=gn_shift[:, 0:1], scale=gn_scale[:, 0:1]).then_inc(
                                         normed_ready_a, 1)

            act.dma_start(ident[:, :], ident_d).then_inc(ident_loaded, 16)
            act.dma_start(small[:, :], small_d).then_inc(small_loaded, 16)
            act.dma_start(columns[:, :], columns_d).then_inc(columns_loaded, 16)
            act.dma_start(constants[:, :], constants_d).then_inc(constants_loaded, 16)
            act.wait_ge(columns_loaded, 16)
            move_xt(0, 0)
            act.wait_ge(weights_ready[0], weights_parts[0])
            move_u(0, 0)
            exponents(0, 0)
            move_probs_a(0, 0)
            move_z(0)
            activate_a(0)
            act.wait_ge(mixer_ready, 3)
            shrink_top(0)
            move_g(0)
            act.wait_ge(weights_ready[2], weights_parts[2])
            act.wait_ge(weights_ready[3], weights_parts[3])

            with act.Fori(0, PAIRS - 1) as j:
                i = j + 1
                move_xt(0, i)
                move_xt(2, j)
                move_u(0, i)
                move_u(2, j)
                exponents(0, i)
                exponents(2, j)
                move_probs_a(0, i)
                move_probs_a(2, j)
                move_z(i)
                activate_a(i)
                square_deviations(j)
                shrink_top(i)
                normalize_a(j)
                move_g(i)
                move_u(3, j)
                exponents(3, j)
                move_probs_a(3, j)

            i = PAIRS - 1
            move_xt(2, i)
            move_u(2, i)
            exponents(2, i)
            move_probs_a(2, i)
            square_deviations(i)
            normalize_a(i)
            move_u(3, i)
            exponents(3, i)
            move_probs_a(3, i)

        @block.vector
        def _(dve):
            def attention_weights(n):
                dve.wait_ge(uw_psum[n], 1)
                b = bank(2, 0 if n == 0 else 1 if n == 2 else 2)
                s = SCALE3 if n == 3 else 1.0
                nc.vector.tensor_scalar(uw[n][:, :], b[:, 0:C + 1], -s, None,
                                        ALU.mult).then_inc(weights_ready[n], 1)
                nc.vector.tensor_scalar(vw[n][:, C:CV], b[:, C + 1:C + 2], s, None,
                                        ALU.mult).then_inc(weights_ready[n], 1)
                nc.vector.tensor_scalar(vb[n][:, C:CV], b[:, C + 2:C + 3], s, None,
                                        ALU.mult).then_inc(weights_ready[n], 1)

            def gated_values(n):
                k = 0 if n == 0 else 1
                gamma = column["gamma0" if n == 0 else "gamma2"]
                nc.vector.tensor_scalar(vw[n][:, 0:C], values[:, k * C:(k + 1) * C], gamma, None,
                                        ALU.mult).then_inc(weights_ready[n], 1)
                nc.vector.tensor_scalar(vb[n][:, 0:C], values[:, (2 + k) * C:(3 + k) * C], gamma,
                                        None, ALU.mult).then_inc(weights_ready[n], 1)

            def output_values():
                b = bank(2, 3)
                nc.vector.tensor_copy(vw[3][:, 0:C], b[:, 0:C]).then_inc(weights_ready[3], 1)
                nc.vector.tensor_tensor(vb[3][:, 0:C], b[:, C:2 * C], values[:, 4 * C:5 * C],
                                        ALU.add).then_inc(attended[3], 1)

            def mixer_weights():
                dve.wait_ge(mixer_psum, 1)
                nc.vector.tensor_copy(mixer[:, :, :].rearrange("p a c -> p (a c)"),
                                      bank(2, 0)).then_inc(mixer_ready, 1)
                for k, sign in ((0, -1.0), (1, 1.0)):
                    nc.vector.tensor_scalar(y_bias[:, k:k + 1], bank(2, 1)[:, 0:1],
                                            column["b2n"], sign * SHRINK, ALU.add,
                                            ALU.add).then_inc(mixer_ready, 1)

            def move_v(n, i):
                dve.wait_ge(v_psum[n], i + 1)
                psum = two_banks(n, 1, TILES * CV).rearrange("p a (t k) -> p a t k", t=TILES)
                bias = vb[n][:, :].unsqueeze(1).unsqueeze(1).to_broadcast([TILE, IMAGES, TILES, CV])
                nc.vector.tensor_tensor(
                    v[n][:, :, :].rearrange("p (a t) k -> p a t k", a=IMAGES), psum, bias,
                    ALU.add).then_inc(v_ready[n], 1)

            def negate_energies(n, i):
                dve.wait_ge(v_ready[n], i + 1)
                for t in range(PT):
                    image, tile = divmod(t, TILES)
                    if tile == 0:
                        dve.wait_ge(energy_psum[n], i * IMAGES + image + 1)
                    nc.vector.tensor_scalar(
                        negated[n][:, t, :],
                        bank(n, 3 * image)[:, tile * TOKENS:(tile + 1) * TOKENS],
                        v[n][:, t, C:CV], FMAX, ALU.subtract, ALU.min,
                        accum_out=lowest[n][:, t:t + 1]).then_inc(negated_ready[n], 1)

            def move_probs_b(n, i):
                dve.wait_ge(probs_t_psum[n], i * IMAGES + 2)
                nc.vector.tensor_copy(probs_t[n][:, 1].rearrange("p m k -> p (m k)"),
                                      bank(n, 2)).then_inc(probs_t_ready_b[n], 1)

            def invert_totals(n, i):
                dve.wait_ge(probs_ready[n], i * PT + PT)
                nc.vector.reciprocal(inverse[n][:, :], total[n][:, :]).then_inc(
                    inverse_ready[n], 1)

            def add_residual(n, i):
                dve.wait_ge(inverse_ready[n], i + 1)
                if n == 3:
                    dve.wait_ge(back_dmas, i * (DMAS * 16) + 16)
                for image in range(IMAGES):
                    dve.wait_ge(mixed_psum[n], i * IMAGES + image + 1)
                    for tile in range(TILES):
                        t = image * TILES + tile
                        op = nc.vector.scalar_tensor_tensor(
                            to[n][:, t, :], bank(n, 3 * image)[:, tile * C:(tile + 1) * C],
                            inverse[n][:, t:t + 1], x_of[n][:, t, :], ALU.mult, ALU.add)
                    op.then_inc(attended[n], 1)

            def activate_b(i):
                dve.wait_ge(w_psum, i * IMAGES + 2)
                b = bank(1, 3)[:, 0:FREQ]
                nc.vector.tensor_scalar(k_act[:, 1, :], b, column["b1k"], 0.0, ALU.add, ALU.max)
                nc.vector.tensor_scalar(n_act[:, 1, :], b, column["b1n"], 0.0, ALU.add,
                                        ALU.max).then_inc(act_ready_b, 1)

            def shrink(i):
                dve.wait_ge(y_top_ready, i + 1)
                nc.vector.scalar_tensor_tensor(
                    y[:, :, :].rearrange("p t k -> p (t k)"), bank(1, 1), y_bias[:, 1:2],
                    y_top[:, :, :].rearrange("p t k -> p (t k)"), ALU.add,
                    ALU.min).then_inc(y_ready, 1)

            def add_bias_image(i):
                dve.wait_ge(back_psum, i + 1)
                nc.vector.tensor_tensor(x2[:, :, :].rearrange("p t k -> p (t k)"), bank(1, 3),
                                        x1[:, :, :].rearrange("p t k -> p (t k)"),
                                        ALU.add).then_inc(x2_ready, 1)

            def channel_stats(i):
                dve.wait_ge(xt_psum[3], i + 1)
                for image in range(IMAGES):
                    op = nc.vector.bn_stats(
                        stats[:, image].rearrange("p e s -> p (e s)"),
                        bank(3, image)[:, 0:TOKENS])
                op.then_inc(stats_ready, 1)

            def channel_spread(i):
                dve.wait_ge(square_ready, i + 1)
                nc.vector.scalar_tensor_tensor(spread[:, :, :], stats[:, :, :, 2], 2.0 / TOKENS,
                                               square[:, :, :], ALU.mult, ALU.add).then_inc(
                                                   spread_ready, 1)
                nc.vector.tensor_tensor(group_mean[:, :], stats[:, :, 0, 1],
                                        bank(3, 3)[:, 0:2 * IMAGES:2],
                                        ALU.subtract).then_inc(group_mean_ready, 1)

            def norm_scales(i):
                dve.wait_ge(variance_psum, i + 1)
                nc.vector.tensor_scalar(group_var[:, :], bank(3, 2)[:, 0:IMAGES], EPS, None,
                                        ALU.add).then_inc(group_var_ready, 1)
                dve.wait_ge(rstd_ready, i + 1)
                nc.vector.tensor_scalar(gn_scale[:, :], rstd[:, :], column["gn_gamma"], None,
                                        ALU.mult).then_inc(gn_scale_ready, 1)
                dve.wait_ge(gn_scale_ready, i + 1)
                dve.wait_ge(group_mean_ready, i + 1)
                nc.vector.tensor_tensor(gn_product[:, :], group_mean[:, :], gn_scale[:, :],
                                        ALU.mult).then_inc(gn_product_ready, 1)
                dve.wait_ge(gn_product_ready, i + 1)
                nc.vector.tensor_scalar(gn_shift[:, :], gn_product[:, :], -1.0,
                                        column["gn_beta"], ALU.mult, ALU.add).then_inc(
                                            gn_shift_ready, 1)

            def normalize_b(i):
                dve.wait_ge(gn_shift_ready, i + 1)
                nc.vector.tensor_scalar(xt[3][:, TILES:PT, :].rearrange("p t k -> p (t k)"),
                                        bank(3, 1)[:, 0:TOKENS], gn_scale[:, 1:2],
                                        gn_shift[:, 1:2], ALU.mult, ALU.add).then_inc(
                                            normed_ready_b, 1)

            dve.wait_ge(values_loaded, 16)
            dve.wait_ge(columns_loaded, 16)
            gated_values(0)
            attention_weights(0)
            gated_values(2)
            attention_weights(2)
            dve.wait_ge(weights_ready[0], weights_parts[0])
            move_v(0, 0)
            negate_energies(0, 0)
            mixer_weights()
            invert_totals(0, 0)
            move_probs_b(0, 0)
            attention_weights(3)
            output_values()
            add_residual(0, 0)
            activate_b(0)
            dve.wait_ge(mixer_ready, 3)
            shrink(0)
            add_bias_image(0)
            dve.wait_ge(weights_ready[2], weights_parts[2])
            dve.wait_ge(weights_ready[3], weights_parts[3])
            dve.wait_ge(attended[3], 1)

            with dve.Fori(0, PAIRS - 1) as j:
                i = j + 1
                move_v(0, i)
                move_v(2, j)
                negate_energies(0, i)
                negate_energies(2, j)
                invert_totals(0, i)
                move_probs_b(0, i)
                invert_totals(2, j)
                move_probs_b(2, j)
                add_residual(0, i)
                add_residual(2, j)
                channel_stats(j)
                activate_b(i)
                channel_spread(j)
                shrink(i)
                norm_scales(j)
                normalize_b(j)
                move_v(3, j)
                negate_energies(3, j)
                add_bias_image(i)
                invert_totals(3, j)
                move_probs_b(3, j)
                add_residual(3, j)

            i = PAIRS - 1
            move_v(2, i)
            negate_energies(2, i)
            invert_totals(2, i)
            move_probs_b(2, i)
            add_residual(2, i)
            channel_stats(i)
            channel_spread(i)
            norm_scales(i)
            normalize_b(i)
            move_v(3, i)
            negate_energies(3, i)
            invert_totals(3, i)
            move_probs_b(3, i)
            add_residual(3, i)


def kernel(**inputs):
    import concourse.bacc as bacc
    from concourse.bass_utils import run_bass_kernel_spmd

    a = {k: np.asarray(t) for k, t in inputs.items()}
    tables = {k: t.astype(np.float32) for k, t in shape_constants().items()}

    def side_by_side(parts):
        return np.ascontiguousarray(np.concatenate(parts, axis=1))

    def small(n):
        bq, bk = a[f"L{n}_conv_bq"], a[f"L{n}_conv_bk"]
        return [a[f"L{n}_conv_Wq"].T, a[f"L{n}_conv_Wk"].T,
                np.broadcast_to(bq[:, None], (CQ, C)), bk[:, None]]

    def rows(bias):
        return np.broadcast_to(bias[None, :], (C, C))

    def stacked(w):
        return w.transpose(1, 2, 0, 3).reshape(C, 2, BS)

    w1, w2 = a["L1_conv_w1"], a["L1_conv_w2"]
    b1, b2 = a["L1_conv_b1"].reshape(2, C), a["L1_conv_b2"].reshape(2, C)
    cols = [b1[0], b1[1], b2[0], b2[1], a["L3_conv_gn_gamma"], a["L3_conv_gn_beta"],
            a["L3_conv_bq"], a["L3_conv_bk"], a["L3_conv_bv"],
            np.broadcast_to(a["L0_conv_gamma"], (C,)), np.broadcast_to(a["L2_conv_gamma"], (C,))]
    arrays = {
        "x": np.ascontiguousarray(a["x"]),
        "ident": tables["ident"],
        "constants": side_by_side([tables[n] for n in CONSTANTS]),
        "small": side_by_side(small(0) + small(2)),
        "values": side_by_side([a["L0_conv_Wv"], a["L2_conv_Wv"], rows(a["L0_conv_bv"]),
                                rows(a["L2_conv_bv"]), rows(a["L3_conv_bo"])]),
        "blocks": np.ascontiguousarray(np.stack(
            [stacked(w1), stacked(w2), stacked(w2.transpose(0, 1, 3, 2))], axis=2)),
        "columns": np.ascontiguousarray(np.stack(cols, axis=1)),
        "layer3": side_by_side([a["L3_conv_wq"].T, a["L3_conv_wk"].T, a["L3_conv_wv"].T,
                                a["L3_conv_wo"]]),
    }
    nc = bacc.Bacc("TRN2", target_bir_lowering=False, num_devices=1)
    args = [nc.dram_tensor(f"in_{n}", t.shape, mybir.dt.float32, kind="ExternalInput").ap()
            for n, t in arrays.items()]
    out = nc.dram_tensor("out", (BATCH, HEIGHT, WIDTH, C), mybir.dt.float32,
                         kind="ExternalOutput").ap()
    build(nc, *args, out)
    r = run_bass_kernel_spmd(nc, [{f"in_{n}": t for n, t in arrays.items()}], core_ids=[0])
    return r.results[0]["out"]
```

```python
from contextlib import ExitStack

import numpy as np

import concourse.bass as bass
from concourse import mybir

BATCH, HEIGHT, WIDTH, C = 8, 16, 16, 128
TOKENS = HEIGHT * WIDTH
TILE = 128
TILES = TOKENS // TILE
IMAGES = 2
PAIRS = BATCH // IMAGES
PT = IMAGES * TILES
CQ = C // 8
CV = C + 1
BLOCKS, BS = 8, 16
GROUPS = 32
SHRINK = 0.01
EPS = 1e-6
SCALE3 = 1.0 / float(np.sqrt(np.float32(C)))
FMAX = 3.0e38

ROW_RUNS = [[(0, 1, 8), (1, 3, 12)], [(4, 4, 5)]]
ROWS = [[h + far * d + k for h, n, d in runs for far in range(2) for k in range(n)]
        for runs in ROW_RUNS]
DMAS = sum(len(runs) for runs in ROW_RUNS)

FIXED = 4
HALF0 = TILE // 2 + FIXED // 2
HALF1 = TILE // 2
WIDE0 = 2 * HALF0
FREQ = WIDE0 + TILE


def frequency_orders():
    forward, backward = [], []
    for rows in ROWS:
        fixed, first, second = [], [], []
        for h in rows:
            for v in range(WIDTH):
                partner = (-h % HEIGHT, -v % WIDTH)
                if partner == (h, v):
                    fixed.append((h, v))
                elif partner not in first:
                    first.append((h, v))
                    second.append(partner)
        f = len(fixed) // 2
        a = fixed[:f] + first + fixed[f:]
        b = fixed[:f] + second + fixed[f:]
        forward.append(a + b)
        backward.append(a[:TILE // 2] + b[f:])
    return forward, backward


def shape_constants():
    def cas(a, n):
        t = 2.0 * np.pi * ((a % n) / n)
        return np.cos(t) + np.sin(t)

    c = np.arange(C)
    eye = np.eye(C)
    forward_order, backward_order = frequency_orders()
    forward, backward = [], []
    for rows, fo, bo in zip(ROWS, forward_order, backward_order):
        tokens = [(h, w) for h in rows for w in range(WIDTH)]
        def table(order):
            return np.array([[cas(w * v, WIDTH) if h == g else 0.0 for g, v in order]
                             for h, w in tokens])
        forward.append(table(fo))
        backward.append(table(bo).T / (WIDTH * C))
    mask = np.kron(np.eye(BLOCKS), np.ones((BS, BS)))
    size = C // GROUPS
    half_average = np.kron(np.eye(GROUPS), np.full((size, size), 0.5 / size))
    return {
        "ident": eye, "cas": cas(np.outer(c, c), C), "forward": np.hstack(forward),
        "backward": np.hstack(backward), "mask": mask, "half_average": half_average,
        "minus_half_average": -half_average, "deviation": eye - half_average,
    }


CONSTANTS = ["cas", "forward", "backward", "mask", "half_average", "minus_half_average",
             "deviation"]
CONSTANT_WIDTHS = [C, FREQ, TILES * TILE, C, C, C, C]
SMALL_WIDTH = 4 * C + 2 * (C + 1)
COLUMNS = ["b1k", "b1n", "b2k", "b2n", "gn_gamma", "gn_beta", "bq3", "bk3", "bv3",
           "gamma0", "gamma2"]


def build(nc, x, ident_d, constants_d, small_d, values_d, blocks_d, columns_d, layer3_d, out):
    fp32 = mybir.dt.float32
    ALU = mybir.AluOpType
    ACT = mybir.ActivationFunctionType

    ctx = ExitStack()
    with ctx:
        def sb(name, shape):
            return ctx.enter_context(nc.sbuf_tensor(name, shape, fp32))

        def sem(name):
            return ctx.enter_context(nc.semaphore(name))

        ident = sb("ident", [C, C])
        constants = sb("constants", [C, sum(CONSTANT_WIDTHS)])
        at, views = 0, {}
        for name, width in zip(CONSTANTS, CONSTANT_WIDTHS):
            views[name] = constants[:, at:at + width]
            at += width
        small = sb("small", [CQ, SMALL_WIDTH])
        values = sb("values", [C, 5 * C])
        blocks = sb("blocks", [C, 2, 3, BS])
        columns = sb("columns", [C, len(COLUMNS)])
        column = {n: columns[:, k:k + 1] for k, n in enumerate(COLUMNS)}
        layer3 = sb("layer3", [C, 4 * C])

        uw = {n: sb(f"uw{n}", [C, C + 1]) for n in (0, 2, 3)}
        vw = {n: sb(f"vw{n}", [C, CV]) for n in (0, 2, 3)}
        vb = {n: sb(f"vb{n}", [C, CV]) for n in (0, 2, 3)}
        bq3_rows = sb("bq3_rows", [C, C])
        bv3_rows = sb("bv3_rows", [C, C])
        half_sum = sb("half_sum", [C, 2, 3, BS])
        sum_dif = sb("sum_dif", [C, 2, 3, BS])
        diagonal = sb("diagonal", [C, 2, 3, C])
        i_plus_b = sb("i_plus_b", [C, C])
        mixer = sb("mixer", [C, 4, C])
        y_bias = sb("y_bias", [C, 2])
        minus_half = sb("minus_half", [C, IMAGES])

        x_in = sb("x_in", [TILE, PT, C])
        x1 = sb("x1", [TILE, PT, C])
        x2 = sb("x2", [TILE, PT, C])
        x3 = sb("x3", [TILE, PT, C])
        x_out = sb("x_out", [TILE, PT, C])
        xt = {n: sb(f"xt{n}", [C, PT, TILE]) for n in (0, 2, 3)}
        u = {n: sb(f"u{n}", [C, PT, TILE]) for n in (0, 2, 3)}
        v = {n: sb(f"v{n}", [TILE, PT, CV]) for n in (0, 2, 3)}
        negated = {n: sb(f"negated{n}", [TILE, PT, TOKENS]) for n in (0, 2, 3)}
        lowest = {n: sb(f"lowest{n}", [TILE, PT]) for n in (0, 2, 3)}
        probs = {n: sb(f"probs{n}", [TILE, PT, TOKENS]) for n in (0, 2, 3)}
        total = {n: sb(f"total{n}", [TILE, PT]) for n in (0, 2, 3)}
        inverse = {n: sb(f"inverse{n}", [TILE, PT]) for n in (0, 2, 3)}
        probs_t = {n: sb(f"probs_t{n}", [TILE, IMAGES, TILES, TOKENS]) for n in (0, 2, 3)}
        z = sb("z", [C, IMAGES, FREQ])
        k_act = sb("k_act", [C, IMAGES, FREQ])
        n_act = sb("n_act", [C, IMAGES, FREQ])
        y_top = sb("y_top", [C, PT, TILE])
        y = sb("y", [C, PT, TILE])
        g = sb("g", [TILE, PT, C])
        stats = sb("stats", [C, IMAGES, 2, 3])
        square = sb("square", [C, IMAGES, 2])
        spread = sb("spread", [C, IMAGES, 2])
        group_mean = sb("group_mean", [C, IMAGES])
        group_var = sb("group_var", [C, IMAGES])
        rstd = sb("rstd", [C, IMAGES])
        gn_scale = sb("gn_scale", [C, IMAGES])
        gn_product = sb("gn_product", [C, IMAGES])
        gn_shift = sb("gn_shift", [C, IMAGES])

        banks = ctx.enter_context(nc.psum_tensor("banks", [128, 8, 512], fp32))
        first_bank = {0: 0, 1: 0, 2: 4, 3: 4}

        def even(layer, image):
            return banks[:, first_bank[layer] + 2 * image, :]

        def odd(layer, image):
            return banks[:, first_bank[layer] + 2 * image + 1, :]

        def spare(k):
            return banks[:, first_bank[2] + k, :]

        ident_loaded = sem("ident_loaded")
        small_loaded = sem("small_loaded")
        values_loaded = sem("values_loaded")
        columns_loaded = sem("columns_loaded")
        blocks_loaded = sem("blocks_loaded")
        constants_loaded = sem("constants_loaded")
        uw_psum = {n: sem(f"uw_psum{n}") for n in (0, 2, 3)}
        weights_ready = {n: sem(f"weights_ready{n}") for n in (0, 2, 3)}
        rows3_ready = sem("rows3_ready")
        halves_made = sem("halves_made")
        diagonal_ready = sem("diagonal_ready")
        mixer_psum = sem("mixer_psum")
        mixer_ready = sem("mixer_ready")
        minus_half_ready = sem("minus_half_ready")

        x_loaded = [sem("x_loaded_a"), sem("x_loaded_b")]
        back_dmas = sem("back_dmas")

        xt_psum = {n: sem(f"xt_psum{n}") for n in (0, 2, 3)}
        xt_ready = {n: sem(f"xt_ready{n}") for n in (0, 2, 3)}
        u_psum = {n: sem(f"u_psum{n}") for n in (0, 2, 3)}
        u_ready = {n: sem(f"u_ready{n}") for n in (0, 2, 3)}
        v_psum = {n: sem(f"v_psum{n}") for n in (0, 2, 3)}
        v_ready = {n: sem(f"v_ready{n}") for n in (0, 2, 3)}
        energy_psum = {n: sem(f"energy_psum{n}") for n in (0, 2, 3)}
        negated_ready = {n: sem(f"negated_ready{n}") for n in (0, 2, 3)}
        probs_ready = {n: sem(f"probs_ready{n}") for n in (0, 2, 3)}
        probs_t_psum = {n: sem(f"probs_t_psum{n}") for n in (0, 2, 3)}
        probs_t_ready = {n: [sem(f"probs_t_ready_a{n}"), sem(f"probs_t_ready_b{n}")]
                         for n in (0, 2, 3)}
        inverse_ready = {n: sem(f"inverse_ready{n}") for n in (0, 2, 3)}
        mixed_psum = {n: sem(f"mixed_psum{n}") for n in (0, 2, 3)}
        attended = {n: sem(f"attended{n}") for n in (0, 2, 3)}

        z_psum, z_ready = sem("z_psum"), sem("z_ready")
        w_psum, act_ready = sem("w_psum"), sem("act_ready")
        y_psum, y_top_ready, y_ready = sem("y_psum"), sem("y_top_ready"), sem("y_ready")
        g_psum, g_ready = sem("g_psum"), sem("g_ready")
        back_psum, x2_ready = sem("back_psum"), sem("x2_ready")

        stats_ready = sem("stats_ready")
        deviation_psum, square_ready = sem("deviation_psum"), sem("square_ready")
        group_mean_ready, spread_ready = sem("group_mean_ready"), sem("spread_ready")
        variance_psum, group_var_ready = sem("variance_psum"), sem("group_var_ready")
        rstd_ready, gn_scale_ready = sem("rstd_ready"), sem("gn_scale_ready")
        gn_product_ready, gn_shift_ready = sem("gn_product_ready"), sem("gn_shift_ready")

        x_of = {0: x_in, 2: x2, 3: x3}
        to = {0: x1, 2: x3, 3: x_out}
        weights_parts = {0: 5, 2: 5, 3: 4}

        def partners(t, image, start, step, length):
            whole = t[:, image, start:start + 1]
            return bass.AP(t, whole.offset, [list(whole.ap[0]), [step, 2], [1, length]])

        def image_of(t, image):
            return t[:, image * TILES:(image + 1) * TILES, :].rearrange("p t k -> p (t k)")

        def halves(flat):
            return flat.rearrange("p (a b) -> p a b", a=2)

        x_tokens = x.rearrange("(i b) h w c -> i b (h w) c", b=IMAGES)
        out_tokens = out.rearrange("(i b) h w c -> i b (h w) c", b=IMAGES)

        def pieces():
            for tile, runs in enumerate(ROW_RUNS):
                p = 0
                for h, n, d in runs:
                    yield tile, p, h * WIDTH, n * WIDTH, d * WIDTH
                    p += 2 * n * WIDTH

        def in_dram(tokens, token, n, d):
            run = tokens[token:token + n]
            return bass.AP(run.tensor, run.offset, [[d * C, 2]] + [list(e) for e in run.ap])

        block = ctx.enter_context(nc.Block())

        @block.sync
        def _(sp):
            def load(i):
                for image in range(IMAGES):
                    if not (isinstance(i, int) and i == 0):
                        sp.wait_ge(attended[0], (i - 1) * IMAGES + image + 1)
                    for tile, p, token, n, d in pieces():
                        sp.dma_start(x_in[p:p + 2 * n, image * TILES + tile, :],
                                     in_dram(x_tokens[i, image], token, n, d)).then_inc(
                                         x_loaded[image], 16)

            def store(i):
                for image in range(IMAGES):
                    sp.wait_ge(attended[3], i * IMAGES + image + 2)
                    for tile, p, token, n, d in pieces():
                        sp.dma_start(in_dram(out_tokens[i, image], token, n, d),
                                     x_out[p:p + 2 * n, image * TILES + tile, :]).then_inc(
                                         back_dmas, 16)

            load(0)
            sp.dma_start(values[:, :], values_d).then_inc(values_loaded, 16)
            sp.dma_start(blocks[:, :, :, :], blocks_d).then_inc(blocks_loaded, 16)
            sp.dma_start(layer3[:, :], layer3_d).then_inc(back_dmas, 16)
            load(1)
            with sp.Fori(0, PAIRS - 2) as j:
                load(j + 2)
                store(j)
            for i in range(PAIRS - 2, PAIRS):
                store(i)
            sp.wait_ge(back_dmas, 16 + BATCH * DMAS * 16)

        @block.gpsimd
        def _(pool):
            pool.memset(minus_half[:, :], -0.5).then_inc(minus_half_ready, 1)
            pool.wait_ge(blocks_loaded, 16)
            pool.tensor_tensor(sum_dif[:, 0], blocks[:, 0], blocks[:, 1],
                               ALU.add).then_inc(halves_made, 1)
            pool.tensor_tensor(sum_dif[:, 1], blocks[:, 0], blocks[:, 1],
                               ALU.subtract).then_inc(halves_made, 1)
            pool.wait_ge(halves_made, 2)
            pool.tensor_scalar(half_sum[:, :, :, :], sum_dif[:, :, :, :], 0.5, None,
                               ALU.mult).then_inc(halves_made, 1)
            pool.wait_ge(halves_made, 3)
            pool.wait_ge(constants_loaded, 16)
            mask = views["mask"].rearrange("p (k o) -> p k o", k=BLOCKS)
            for part in range(2):
                for which in range(3):
                    pool.tensor_tensor(
                        diagonal[:, part, which].rearrange("p (k o) -> p k o", k=BLOCKS), mask,
                        half_sum[:, part, which].unsqueeze(1).to_broadcast([C, BLOCKS, BS]),
                        ALU.mult).then_inc(diagonal_ready, 1)
            pool.wait_ge(diagonal_ready, 6)
            pool.wait_ge(ident_loaded, 16)
            pool.tensor_tensor(i_plus_b[:, :], diagonal[:, 1, 1], ident[:, :],
                               ALU.add).then_inc(diagonal_ready, 1)
            pool.wait_ge(columns_loaded, 16)
            for rows, name in ((bq3_rows, "bq3"), (bv3_rows, "bv3")):
                pool.tensor_copy(rows[:, :], column[name].to_broadcast([C, C])).then_inc(
                    rows3_ready, 1)
            pool.wait_ge(minus_half_ready, 1)
            with pool.Fori(0, PAIRS) as i:
                pool.wait_ge(group_var_ready, i + 1)
                pool.tensor_tensor(rstd[:, :], group_var[:, :], minus_half[:, :],
                                   ALU.pow).then_inc(rstd_ready, 1)

        @block.tensor
        def _(pe):
            def small_products(n, base):
                b = spare(0 if n == 0 else 1 if n == 2 else 2)
                if n == 3:
                    wq_t, wk_t = layer3[:, 0:C], layer3[:, C:2 * C]
                    bq, bk, bq_rows = column["bq3"], column["bk3"], bq3_rows[:, :]
                else:
                    wq_t, wk_t = small[:, base:base + C], small[:, base + C:base + 2 * C]
                    bq_rows = small[:, base + 2 * C:base + 3 * C]
                    bq, bk = bq_rows[:, 0:1], small[:, base + 3 * C:base + 3 * C + 1]
                nc.tensor.matmul(b[:, 0:C], wq_t, wk_t, start=True, stop=True)
                nc.tensor.matmul(b[:, C:C + 1], wk_t, bq, start=True, stop=True)
                nc.tensor.matmul(b[:, C + 1:C + 2], wq_t, bk, start=True, stop=True)
                return nc.tensor.matmul(b[:, C + 2:C + 3], bq_rows, bk, start=True, stop=True)

            def setup_02():
                pe.wait_ge(small_loaded, 16)
                small_products(0, 0).then_inc(uw_psum[0], 1)
                small_products(2, 3 * C + 1).then_inc(uw_psum[2], 1)

            def setup_3():
                pe.wait_ge(back_dmas, 16)
                pe.wait_ge(columns_loaded, 16)
                pe.wait_ge(rows3_ready, 2)
                small_products(3, 0)
                wv_t, wo = layer3[:, 2 * C:3 * C], layer3[:, 3 * C:4 * C]
                nc.tensor.matmul(spare(3)[:, 0:C], wv_t, wo, start=True, stop=True)
                nc.tensor.matmul(spare(3)[:, C:2 * C], bv3_rows[:, :], wo,
                                 start=True, stop=True).then_inc(uw_psum[3], 1)

            def setup_1():
                pe.wait_ge(diagonal_ready, 7)
                pe.wait_ge(weights_ready[0], weights_parts[0])
                pe.wait_ge(weights_ready[2], weights_parts[2])
                b = spare(0)
                cas = views["cas"]
                a2, a2_t, b2_t = diagonal[:, 0, 1], diagonal[:, 0, 2], diagonal[:, 1, 2]
                nc.tensor.matmul(b[:, 0:C], cas, diagonal[:, 0, 0], start=True, stop=True)
                nc.tensor.matmul(b[:, C:2 * C], cas, diagonal[:, 1, 0], start=True, stop=True)
                nc.tensor.matmul(b[:, 2 * C:3 * C], a2_t, i_plus_b[:, :], start=True, stop=True)
                nc.tensor.matmul(b[:, 3 * C:4 * C], b2_t, i_plus_b[:, :], start=True, stop=False)
                nc.tensor.matmul(b[:, 3 * C:4 * C], ident[:, :], a2, start=False, stop=True)
                nc.tensor.matmul(spare(1)[:, 0:1], i_plus_b[:, :], column["b2k"],
                                 start=True, stop=True).then_inc(mixer_psum, 1)

            def transpose_x(n, i):
                for image in range(IMAGES):
                    if n == 0:
                        pe.wait_ge(x_loaded[image], (i + 1) * (DMAS * 16))
                        if not (isinstance(i, int) and i == 0):
                            pe.wait_ge(x2_ready, (i - 1) * IMAGES + image + 1)
                    elif n == 2:
                        pe.wait_ge(x2_ready, i * IMAGES + image + 1)
                    else:
                        pe.wait_ge(attended[2], i * IMAGES + image + 1)
                    for tile in range(TILES):
                        mm = nc.tensor.transpose(even(n, image)[:, tile * TILE:(tile + 1) * TILE],
                                                 x_of[n][:, image * TILES + tile, :], ident[:, :])
                    mm.then_inc(xt_psum[n], 1)

            def project(n, i):
                for image in range(IMAGES):
                    pe.wait_ge(xt_ready[n], i * IMAGES + image + 1)
                    if n == 2 and image == 0:
                        pe.wait_ge(attended[3], i * IMAGES + 1)
                    nc.tensor.matmul(odd(n, image)[:, 0:TOKENS], uw[n][:, 0:C],
                                     xt[n][:, image * TILES:(image + 1) * TILES, :],
                                     start=True, stop=True).then_inc(u_psum[n], 1)
                    for tile in range(TILES):
                        mm = nc.tensor.matmul(even(n, image)[:, tile * CV:(tile + 1) * CV],
                                              xt[n][:, image * TILES + tile, :], vw[n][:, :],
                                              start=True, stop=True)
                    mm.then_inc(v_psum[n], 1)

            def energies(n, i):
                for image in range(IMAGES):
                    pe.wait_ge(u_ready[n], i * IMAGES + image + 1)
                    for tile in range(TILES):
                        mm = nc.tensor.matmul(
                            odd(n, image)[:, tile * TOKENS:(tile + 1) * TOKENS],
                            u[n][:, image * TILES + tile, :],
                            xt[n][:, image * TILES:(image + 1) * TILES, :],
                            start=True, stop=True)
                    mm.then_inc(energy_psum[n], 1)

            def transpose_probs(n, i):
                for image in range(IMAGES):
                    pe.wait_ge(v_ready[n], i * IMAGES + image + 1)
                    pe.wait_ge(probs_ready[n], i * PT + (image + 1) * TILES)
                    for m in range(TILES):
                        for tile in range(TILES):
                            at = m * TOKENS + tile * TILE
                            mm = nc.tensor.transpose(
                                even(n, image)[:, at:at + TILE],
                                probs[n][:, image * TILES + tile, m * TILE:(m + 1) * TILE],
                                ident[:, :])
                    mm.then_inc(probs_t_psum[n], 1)

            def mix_values(n, i):
                for image in range(IMAGES):
                    pe.wait_ge(probs_t_ready[n][image], i + 1)
                    for tile in range(TILES):
                        for m in range(TILES):
                            mm = nc.tensor.matmul(
                                odd(n, image)[:, tile * C:(tile + 1) * C],
                                probs_t[n][:, image, m, tile * TILE:(tile + 1) * TILE],
                                v[n][:, image * TILES + m, 0:C],
                                start=(m == 0), stop=(m == TILES - 1))
                    mm.then_inc(mixed_psum[n], 1)

            def forward_tokens(i):
                for image in range(IMAGES):
                    pe.wait_ge(attended[0], i * IMAGES + image + 1)
                    b = even(1, image)
                    nc.tensor.matmul(b[:, 0:WIDE0], x1[:, image * TILES, :],
                                     views["forward"][:, 0:WIDE0], start=True, stop=True)
                    nc.tensor.matmul(b[:, WIDE0:FREQ], x1[:, image * TILES + 1, :],
                                     views["forward"][:, WIDE0:FREQ],
                                     start=True, stop=True).then_inc(z_psum, 1)

            def first_product(i):
                for image in range(IMAGES):
                    pe.wait_ge(z_ready, i * IMAGES + image + 1)
                    b = odd(1, image)
                    nc.tensor.matmul(b[:, 0:FREQ], mixer[:, 0], z[:, image, :],
                                     start=True, stop=False)
                    nc.tensor.matmul(halves(b[:, 0:WIDE0]), mixer[:, 1],
                                     partners(z, image, HALF0, -HALF0, HALF0),
                                     start=False, stop=False)
                    nc.tensor.matmul(halves(b[:, WIDE0:FREQ]), mixer[:, 1],
                                     partners(z, image, WIDE0 + HALF1, -HALF1, HALF1),
                                     start=False, stop=True).then_inc(w_psum, 1)

            def second_product(i):
                skip = HALF0 + FIXED // 2
                for image in range(IMAGES):
                    pe.wait_ge(act_ready, i * IMAGES + image + 1)
                    own = [partners(k_act, image, 0, skip, TILE // 2),
                           partners(k_act, image, WIDE0, HALF1, HALF1)]
                    other = [partners(n_act, image, HALF0, FIXED // 2 - HALF0, TILE // 2),
                             partners(n_act, image, WIDE0 + HALF1, -HALF1, HALF1)]
                    for tile in range(TILES):
                        o = halves(even(1, image)[:, tile * TILE:(tile + 1) * TILE])
                        nc.tensor.matmul(o, mixer[:, 2], own[tile], start=True, stop=False)
                        mm = nc.tensor.matmul(o, mixer[:, 3], other[tile], start=False, stop=True)
                    mm.then_inc(y_psum, 1)

            def backward_channels(i):
                for image in range(IMAGES):
                    pe.wait_ge(y_ready, i * IMAGES + image + 1)
                    for tile in range(TILES):
                        mm = nc.tensor.matmul(odd(1, image)[:, tile * C:(tile + 1) * C],
                                              y[:, image * TILES + tile, :], views["cas"],
                                              start=True, stop=True)
                    mm.then_inc(g_psum, 1)

            def backward_tokens(i):
                for image in range(IMAGES):
                    pe.wait_ge(g_ready, i * IMAGES + image + 1)
                    for tile in range(TILES):
                        mm = nc.tensor.matmul(
                            even(1, image)[:, tile * C:(tile + 1) * C],
                            views["backward"][:, tile * TILE:(tile + 1) * TILE],
                            g[:, image * TILES + tile, :], start=True, stop=True)
                    mm.then_inc(back_psum, 1)

            def group_deviations(i):
                pe.wait_ge(stats_ready, i + 1)
                b = odd(3, 0)[:, 0:2 * IMAGES].rearrange("p (a e) -> p a e", a=IMAGES)
                means = stats[:, :, :, 1]
                others = bass.AP(stats, stats[:, :, 1, 1].offset,
                                 [list(means.ap[0]), list(means.ap[1]), [-means.ap[2][0], 2]])
                nc.tensor.matmul(b, views["deviation"], means, start=True, stop=False)
                nc.tensor.matmul(b, views["minus_half_average"], others,
                                 start=False, stop=True).then_inc(deviation_psum, 1)

            def group_variances(i):
                pe.wait_ge(spread_ready, i + 1)
                b = odd(3, 1)[:, 0:IMAGES]
                nc.tensor.matmul(b, views["half_average"], spread[:, :, 0],
                                 start=True, stop=False)
                nc.tensor.matmul(b, views["half_average"], spread[:, :, 1],
                                 start=False, stop=True).then_inc(variance_psum, 1)

            pe.wait_ge(ident_loaded, 16)
            setup_02()
            transpose_x(0, 0)
            pe.wait_ge(weights_ready[0], weights_parts[0])
            project(0, 0)
            energies(0, 0)
            setup_1()
            transpose_probs(0, 0)
            setup_3()
            mix_values(0, 0)
            forward_tokens(0)
            pe.wait_ge(mixer_ready, 3)
            first_product(0)
            second_product(0)
            backward_channels(0)
            backward_tokens(0)
            pe.wait_ge(weights_ready[3], weights_parts[3])

            with pe.Fori(0, PAIRS - 1) as j:
                i = j + 1
                transpose_x(0, i)
                transpose_x(2, j)
                project(0, i)
                project(2, j)
                energies(2, j)
                energies(0, i)
                transpose_probs(2, j)
                transpose_probs(0, i)
                mix_values(2, j)
                transpose_x(3, j)
                mix_values(0, i)
                group_deviations(j)
                forward_tokens(i)
                group_variances(j)
                first_product(i)
                second_product(i)
                project(3, j)
                backward_channels(i)
                energies(3, j)
                backward_tokens(i)
                transpose_probs(3, j)
                mix_values(3, j)

            i = PAIRS - 1
            transpose_x(2, i)
            project(2, i)
            energies(2, i)
            transpose_probs(2, i)
            mix_values(2, i)
            transpose_x(3, i)
            group_deviations(i)
            group_variances(i)
            project(3, i)
            energies(3, i)
            transpose_probs(3, i)
            mix_values(3, i)

        @block.scalar
        def _(act):
            def move_xt(n, i):
                for image in range(IMAGES):
                    act.wait_ge(xt_psum[n], i * IMAGES + image + 1)
                    nc.scalar.activation(image_of(xt[n], image), even(n, image)[:, 0:TOKENS],
                                         ACT.Copy).then_inc(xt_ready[n], 1)

            def move_u(n, i):
                for image in range(IMAGES):
                    act.wait_ge(u_psum[n], i * IMAGES + image + 1)
                    nc.scalar.activation(image_of(u[n], image), odd(n, image)[:, 0:TOKENS],
                                         ACT.Identity, bias=uw[n][:, C:C + 1]).then_inc(
                                             u_ready[n], 1)

            def exponents(n, i):
                for t in range(PT):
                    act.wait_ge(negated_ready[n], i * PT + t + 1)
                    nc.scalar.activation(probs[n][:, t, :], negated[n][:, t, :], ACT.Exp,
                                         bias=lowest[n][:, t:t + 1], scale=-1.0,
                                         accum_out=total[n][:, t:t + 1]).then_inc(
                                             probs_ready[n], 1)

            def move_probs_a(n, i):
                act.wait_ge(probs_t_psum[n], i * IMAGES + 1)
                nc.scalar.activation(probs_t[n][:, 0].rearrange("p m k -> p (m k)"), even(n, 0),
                                     ACT.Copy).then_inc(probs_t_ready[n][0], 1)

            def move_z(i):
                for image in range(IMAGES):
                    act.wait_ge(z_psum, i * IMAGES + image + 1)
                    nc.scalar.activation(z[:, image, :], even(1, image)[:, 0:FREQ],
                                         ACT.Copy).then_inc(z_ready, 1)

            def activate(i):
                for image in range(IMAGES):
                    act.wait_ge(w_psum, i * IMAGES + image + 1)
                    b = odd(1, image)[:, 0:FREQ]
                    nc.scalar.activation(k_act[:, image, :], b, ACT.Relu, bias=column["b1k"])
                    nc.scalar.activation(n_act[:, image, :], b, ACT.Relu,
                                         bias=column["b1n"]).then_inc(act_ready, 1)

            def shrink_top(i):
                for image in range(IMAGES):
                    act.wait_ge(y_psum, i * IMAGES + image + 1)
                    nc.scalar.activation(image_of(y_top, image), even(1, image)[:, 0:TOKENS],
                                         ACT.Relu, bias=y_bias[:, 0:1]).then_inc(y_top_ready, 1)

            def move_g(i):
                for image in range(IMAGES):
                    act.wait_ge(g_psum, i * IMAGES + image + 1)
                    nc.scalar.activation(image_of(g, image), odd(1, image)[:, 0:TOKENS],
                                         ACT.Copy).then_inc(g_ready, 1)

            def square_deviations(i):
                act.wait_ge(deviation_psum, i + 1)
                nc.scalar.activation(square[:, :, :].rearrange("p a e -> p (a e)"),
                                     odd(3, 0)[:, 0:2 * IMAGES], ACT.Square).then_inc(
                                         square_ready, 1)

            def normalize(i):
                act.wait_ge(gn_shift_ready, i + 1)
                for image in range(IMAGES):
                    nc.scalar.activation(image_of(xt[3], image), even(3, image)[:, 0:TOKENS],
                                         ACT.Identity, bias=gn_shift[:, image:image + 1],
                                         scale=gn_scale[:, image:image + 1]).then_inc(
                                             xt_ready[3], 1)

            act.dma_start(ident[:, :], ident_d).then_inc(ident_loaded, 16)
            act.dma_start(small[:, :], small_d).then_inc(small_loaded, 16)
            act.dma_start(columns[:, :], columns_d).then_inc(columns_loaded, 16)
            act.dma_start(constants[:, :], constants_d).then_inc(constants_loaded, 16)
            act.wait_ge(columns_loaded, 16)
            move_xt(0, 0)
            act.wait_ge(weights_ready[0], weights_parts[0])
            move_u(0, 0)
            exponents(0, 0)
            move_probs_a(0, 0)
            move_z(0)
            activate(0)
            act.wait_ge(mixer_ready, 3)
            shrink_top(0)
            move_g(0)
            act.wait_ge(weights_ready[2], weights_parts[2])
            act.wait_ge(weights_ready[3], weights_parts[3])

            with act.Fori(0, PAIRS - 1) as j:
                i = j + 1
                move_xt(0, i)
                move_xt(2, j)
                move_u(0, i)
                move_u(2, j)
                exponents(2, j)
                exponents(0, i)
                move_probs_a(2, j)
                move_probs_a(0, i)
                square_deviations(j)
                move_z(i)
                activate(i)
                normalize(j)
                shrink_top(i)
                move_u(3, j)
                move_g(i)
                exponents(3, j)
                move_probs_a(3, j)

            i = PAIRS - 1
            move_xt(2, i)
            move_u(2, i)
            exponents(2, i)
            move_probs_a(2, i)
            square_deviations(i)
            normalize(i)
            move_u(3, i)
            exponents(3, i)
            move_probs_a(3, i)

        @block.vector
        def _(dve):
            def attention_weights(n):
                dve.wait_ge(uw_psum[n], 1)
                b = spare(0 if n == 0 else 1 if n == 2 else 2)
                s = SCALE3 if n == 3 else 1.0
                nc.vector.tensor_scalar(uw[n][:, :], b[:, 0:C + 1], -s, None,
                                        ALU.mult).then_inc(weights_ready[n], 1)
                nc.vector.tensor_scalar(vw[n][:, C:CV], b[:, C + 1:C + 2], s, None,
                                        ALU.mult).then_inc(weights_ready[n], 1)
                nc.vector.tensor_scalar(vb[n][:, C:CV], b[:, C + 2:C + 3], s, None,
                                        ALU.mult).then_inc(weights_ready[n], 1)

            def gated_values(n):
                k = 0 if n == 0 else 1
                gamma = column["gamma0" if n == 0 else "gamma2"]
                nc.vector.tensor_scalar(vw[n][:, 0:C], values[:, k * C:(k + 1) * C], gamma, None,
                                        ALU.mult).then_inc(weights_ready[n], 1)
                nc.vector.tensor_scalar(vb[n][:, 0:C], values[:, (2 + k) * C:(3 + k) * C], gamma,
                                        None, ALU.mult).then_inc(weights_ready[n], 1)

            def output_values():
                b = spare(3)
                nc.vector.tensor_copy(vw[3][:, 0:C], b[:, 0:C]).then_inc(weights_ready[3], 1)
                nc.vector.tensor_tensor(vb[3][:, 0:C], b[:, C:2 * C], values[:, 4 * C:5 * C],
                                        ALU.add).then_inc(attended[3], 1)

            def mixer_weights():
                dve.wait_ge(mixer_psum, 1)
                nc.vector.tensor_copy(mixer[:, :, :].rearrange("p a c -> p (a c)"),
                                      spare(0)).then_inc(mixer_ready, 1)
                for k, sign in ((0, -1.0), (1, 1.0)):
                    nc.vector.tensor_scalar(y_bias[:, k:k + 1], spare(1)[:, 0:1],
                                            column["b2n"], sign * SHRINK, ALU.add,
                                            ALU.add).then_inc(mixer_ready, 1)

            def move_v(n, i):
                bias = vb[n][:, :].unsqueeze(1).to_broadcast([TILE, TILES, CV])
                for image in range(IMAGES):
                    dve.wait_ge(v_psum[n], i * IMAGES + image + 1)
                    nc.vector.tensor_tensor(
                        v[n][:, image * TILES:(image + 1) * TILES, :],
                        even(n, image)[:, 0:TILES * CV].rearrange("p (t k) -> p t k", t=TILES),
                        bias, ALU.add).then_inc(v_ready[n], 1)

            def negate_energies(n, i):
                for image in range(IMAGES):
                    dve.wait_ge(v_ready[n], i * IMAGES + image + 1)
                    dve.wait_ge(energy_psum[n], i * IMAGES + image + 1)
                    for tile in range(TILES):
                        t = image * TILES + tile
                        nc.vector.tensor_scalar(
                            negated[n][:, t, :],
                            odd(n, image)[:, tile * TOKENS:(tile + 1) * TOKENS],
                            v[n][:, t, C:CV], FMAX, ALU.subtract, ALU.min,
                            accum_out=lowest[n][:, t:t + 1]).then_inc(negated_ready[n], 1)

            def move_probs_b(n, i):
                dve.wait_ge(probs_t_psum[n], i * IMAGES + 2)
                nc.vector.tensor_copy(probs_t[n][:, 1].rearrange("p m k -> p (m k)"),
                                      even(n, 1)).then_inc(probs_t_ready[n][1], 1)

            def invert_totals(n, i):
                for image in range(IMAGES):
                    dve.wait_ge(probs_ready[n], i * PT + (image + 1) * TILES)
                    at = slice(image * TILES, (image + 1) * TILES)
                    nc.vector.reciprocal(inverse[n][:, at], total[n][:, at]).then_inc(
                        inverse_ready[n], 1)

            def add_residual(n, i):
                if n == 3:
                    dve.wait_ge(back_dmas, i * (IMAGES * DMAS * 16) + 16)
                for image in range(IMAGES):
                    dve.wait_ge(inverse_ready[n], i * IMAGES + image + 1)
                    dve.wait_ge(mixed_psum[n], i * IMAGES + image + 1)
                    for tile in range(TILES):
                        t = image * TILES + tile
                        op = nc.vector.scalar_tensor_tensor(
                            to[n][:, t, :], odd(n, image)[:, tile * C:(tile + 1) * C],
                            inverse[n][:, t:t + 1], x_of[n][:, t, :], ALU.mult, ALU.add)
                    op.then_inc(attended[n], 1)

            def shrink(i):
                for image in range(IMAGES):
                    dve.wait_ge(y_top_ready, i * IMAGES + image + 1)
                    nc.vector.scalar_tensor_tensor(
                        image_of(y, image), even(1, image)[:, 0:TOKENS], y_bias[:, 1:2],
                        image_of(y_top, image), ALU.add, ALU.min).then_inc(y_ready, 1)

            def add_bias_image(i):
                for image in range(IMAGES):
                    dve.wait_ge(back_psum, i * IMAGES + image + 1)
                    nc.vector.tensor_tensor(image_of(x2, image), even(1, image)[:, 0:TOKENS],
                                            image_of(x1, image), ALU.add).then_inc(x2_ready, 1)

            def channel_stats(i):
                for image in range(IMAGES):
                    dve.wait_ge(xt_psum[3], i * IMAGES + image + 1)
                    op = nc.vector.bn_stats(stats[:, image].rearrange("p e s -> p (e s)"),
                                            even(3, image)[:, 0:TOKENS])
                op.then_inc(stats_ready, 1)

            def channel_spread(i):
                dve.wait_ge(square_ready, i + 1)
                nc.vector.scalar_tensor_tensor(spread[:, :, :], stats[:, :, :, 2], 2.0 / TOKENS,
                                               square[:, :, :], ALU.mult, ALU.add).then_inc(
                                                   spread_ready, 1)
                nc.vector.tensor_tensor(group_mean[:, :], stats[:, :, 0, 1],
                                        odd(3, 0)[:, 0:2 * IMAGES:2],
                                        ALU.subtract).then_inc(group_mean_ready, 1)

            def norm_scales(i):
                dve.wait_ge(variance_psum, i + 1)
                nc.vector.tensor_scalar(group_var[:, :], odd(3, 1)[:, 0:IMAGES], EPS, None,
                                        ALU.add).then_inc(group_var_ready, 1)
                dve.wait_ge(rstd_ready, i + 1)
                nc.vector.tensor_scalar(gn_scale[:, :], rstd[:, :], column["gn_gamma"], None,
                                        ALU.mult).then_inc(gn_scale_ready, 1)
                dve.wait_ge(gn_scale_ready, i + 1)
                dve.wait_ge(group_mean_ready, i + 1)
                nc.vector.tensor_tensor(gn_product[:, :], group_mean[:, :], gn_scale[:, :],
                                        ALU.mult).then_inc(gn_product_ready, 1)
                dve.wait_ge(gn_product_ready, i + 1)
                nc.vector.tensor_scalar(gn_shift[:, :], gn_product[:, :], -1.0,
                                        column["gn_beta"], ALU.mult, ALU.add).then_inc(
                                            gn_shift_ready, 1)

            dve.wait_ge(values_loaded, 16)
            dve.wait_ge(columns_loaded, 16)
            gated_values(0)
            attention_weights(0)
            gated_values(2)
            attention_weights(2)
            dve.wait_ge(weights_ready[0], weights_parts[0])
            move_v(0, 0)
            negate_energies(0, 0)
            mixer_weights()
            invert_totals(0, 0)
            move_probs_b(0, 0)
            attention_weights(3)
            output_values()
            add_residual(0, 0)
            dve.wait_ge(mixer_ready, 3)
            shrink(0)
            add_bias_image(0)
            dve.wait_ge(weights_ready[2], weights_parts[2])
            dve.wait_ge(weights_ready[3], weights_parts[3])
            dve.wait_ge(attended[3], 1)

            with dve.Fori(0, PAIRS - 1) as j:
                i = j + 1
                move_v(0, i)
                move_v(2, j)
                negate_energies(2, j)
                negate_energies(0, i)
                invert_totals(2, j)
                invert_totals(0, i)
                move_probs_b(2, j)
                move_probs_b(0, i)
                add_residual(2, j)
                channel_stats(j)
                add_residual(0, i)
                channel_spread(j)
                norm_scales(j)
                shrink(i)
                move_v(3, j)
                negate_energies(3, j)
                invert_totals(3, j)
                add_bias_image(i)
                move_probs_b(3, j)
                add_residual(3, j)

            i = PAIRS - 1
            move_v(2, i)
            negate_energies(2, i)
            invert_totals(2, i)
            move_probs_b(2, i)
            add_residual(2, i)
            channel_stats(i)
            channel_spread(i)
            norm_scales(i)
            move_v(3, i)
            negate_energies(3, i)
            invert_totals(3, i)
            move_probs_b(3, i)
            add_residual(3, i)


def kernel(**inputs):
    import concourse.bacc as bacc
    from concourse.bass_utils import run_bass_kernel_spmd

    a = {k: np.asarray(t) for k, t in inputs.items()}
    tables = {k: t.astype(np.float32) for k, t in shape_constants().items()}

    def side_by_side(parts):
        return np.ascontiguousarray(np.concatenate(parts, axis=1))

    def small(n):
        bq, bk = a[f"L{n}_conv_bq"], a[f"L{n}_conv_bk"]
        return [a[f"L{n}_conv_Wq"].T, a[f"L{n}_conv_Wk"].T,
                np.broadcast_to(bq[:, None], (CQ, C)), bk[:, None]]

    def rows(bias):
        return np.broadcast_to(bias[None, :], (C, C))

    def stacked(w):
        return w.transpose(1, 2, 0, 3).reshape(C, 2, BS)

    w1, w2 = a["L1_conv_w1"], a["L1_conv_w2"]
    b1, b2 = a["L1_conv_b1"].reshape(2, C), a["L1_conv_b2"].reshape(2, C)
    cols = [b1[0], b1[1], b2[0], b2[1], a["L3_conv_gn_gamma"], a["L3_conv_gn_beta"],
            a["L3_conv_bq"], a["L3_conv_bk"], a["L3_conv_bv"],
            np.broadcast_to(a["L0_conv_gamma"], (C,)), np.broadcast_to(a["L2_conv_gamma"], (C,))]
    arrays = {
        "x": np.ascontiguousarray(a["x"]),
        "ident": tables["ident"],
        "constants": side_by_side([tables[n] for n in CONSTANTS]),
        "small": side_by_side(small(0) + small(2)),
        "values": side_by_side([a["L0_conv_Wv"], a["L2_conv_Wv"], rows(a["L0_conv_bv"]),
                                rows(a["L2_conv_bv"]), rows(a["L3_conv_bo"])]),
        "blocks": np.ascontiguousarray(np.stack(
            [stacked(w1), stacked(w2), stacked(w2.transpose(0, 1, 3, 2))], axis=2)),
        "columns": np.ascontiguousarray(np.stack(cols, axis=1)),
        "layer3": side_by_side([a["L3_conv_wq"].T, a["L3_conv_wk"].T, a["L3_conv_wv"].T,
                                a["L3_conv_wo"]]),
    }
    nc = bacc.Bacc("TRN2", target_bir_lowering=False, num_devices=1)
    args = [nc.dram_tensor(f"in_{n}", t.shape, mybir.dt.float32, kind="ExternalInput").ap()
            for n, t in arrays.items()]
    out = nc.dram_tensor("out", (BATCH, HEIGHT, WIDTH, C), mybir.dt.float32,
                         kind="ExternalOutput").ap()
    build(nc, *args, out)
    r = run_bass_kernel_spmd(nc, [{f"in_{n}": t for n, t in arrays.items()}], core_ids=[0])
    return r.results[0]["out"]
```

```python
from collections import namedtuple
from contextlib import ExitStack

import numpy as np

import concourse.bass as bass
from concourse import mybir

BATCH, HEIGHT, WIDTH, C = 8, 16, 16, 128
TOKENS = HEIGHT * WIDTH
TILE = 128
TILES = TOKENS // TILE
LAYERS = 4
MIXER, NORMED = 1, 3
CQ = C // 8
CV = C + 1
BLOCKS, BS = 8, 16
GROUPS = 32
SHRINK = 0.01
WARM_UP = 6
EPS = 1e-6
SCALE3 = 1.0 / float(np.sqrt(np.float32(C)))
FMAX = 3.0e38

ROW_RUNS = [[(0, 1, 8), (1, 3, 12)], [(4, 4, 5)]]
ROWS = [[h + far * d + k for h, n, d in runs for far in range(2) for k in range(n)]
        for runs in ROW_RUNS]
DMAS = sum(len(runs) for runs in ROW_RUNS)

LOADS = [(0, 1), (1, 2), (2, BATCH)]

FIXED = 4
HALF = (TILE // 2 + FIXED // 2, TILE // 2)
SUMS = sum(HALF)
FREQ = 2 * SUMS


def frequency_orders():
    pairs, backward = [], []
    for rows in ROWS:
        fixed, first, second = [], [], []
        for h in rows:
            for v in range(WIDTH):
                partner = (-h % HEIGHT, -v % WIDTH)
                if partner == (h, v):
                    fixed.append((h, v))
                elif partner not in first:
                    first.append((h, v))
                    second.append(partner)
        f = len(fixed) // 2
        a = fixed[:f] + first + fixed[f:]
        b = fixed[:f] + second + fixed[f:]
        pairs.append((a, b))
        backward.append(a[:TILE // 2] + b[f:])
    return pairs, backward


def shape_constants():
    def cas(a, n):
        t = 2.0 * np.pi * ((a % n) / n)
        return np.cos(t) + np.sin(t)

    c = np.arange(C)
    eye = np.eye(C)
    pairs, backward_order = frequency_orders()
    forward, backward = [], []
    for rows, (first, second), order in zip(ROWS, pairs, backward_order):
        tokens = [(h, w) for h in rows for w in range(WIDTH)]
        def table(order):
            return np.array([[cas(w * v, WIDTH) if h == g else 0.0 for g, v in order]
                             for h, w in tokens])
        forward += [(table(first) + table(second)) / 2, (table(first) - table(second)) / 2]
        backward.append(table(order).T / (WIDTH * C))
    mask = np.kron(np.eye(BLOCKS), np.ones((BS, BS)))
    size = C // GROUPS
    half_average = np.kron(np.eye(GROUPS), np.full((size, size), 0.5 / size))
    return {
        "ident": eye, "cas": cas(np.outer(c, c), C), "forward": np.hstack(forward),
        "backward": np.hstack(backward), "mask": mask, "half_average": half_average,
    }


CONSTANTS = ["cas", "forward", "backward", "mask", "half_average"]
CONSTANT_WIDTHS = [C, FREQ, TILES * TILE, C, C]

Job = namedtuple("Job", "layer image half")


def job_at(slot, back):
    layer, image, half = slot[0], slot[1] - back, (slot[2] - back) % 2
    if isinstance(slot[1], int):
        if image < 0:
            layer, image = layer - 1, image + BATCH
        elif image >= BATCH:
            layer, image = layer + 1, image - BATCH
    return Job(layer, image, half) if 0 <= layer < LAYERS else None


def attends(job):
    return job is not None and job.layer != MIXER


def mixes(job):
    return job is not None and job.layer == MIXER


def norms(job):
    return job is not None and job.layer == NORMED


def is_job(job, layer, image):
    return isinstance(job.image, int) and job[:2] == (layer, image)


def in_order(engine, slot):
    for layer in range(LAYERS):
        head = 3 if layer == MIXER else 2
        tail = 1 if layer == MIXER else 2 if layer >= NORMED - 1 else 0
        for image in range(head):
            slot(Job(layer, image, image % 2))
        with engine.Fori(head // 2, (BATCH - tail) // 2) as pair:
            for odd in range(2):
                slot(Job(layer, pair * 2 + (head % 2 + odd), (head + odd) % 2))
        for image in range(BATCH - tail, BATCH):
            slot(Job(layer, image, image % 2))
    for image in range(BATCH, BATCH + 2):
        slot(Job(LAYERS - 1, image, image % 2))


SMALL_AT = {0: 0, 2: 3 * C + 1}
SMALL_WIDTH = 2 * (3 * C + 1)
COLUMNS = ["b1k", "b1n", "b2k", "b2n", "gn_gamma", "gn_beta", "bq3", "bv3",
           "gamma0", "gamma2"]


def build(nc, x, ident_columns_d, constants_d, small_d, values_d, blocks_d, layer3_d, out):
    fp32 = mybir.dt.float32
    ALU = mybir.AluOpType
    ACT = mybir.ActivationFunctionType

    ctx = ExitStack()
    with ctx:
        def sb(name, shape):
            return ctx.enter_context(nc.sbuf_tensor(name, shape, fp32))

        def sem(name):
            return ctx.enter_context(nc.semaphore(name))

        ident_columns = sb("ident_columns", [C, C + len(COLUMNS)])
        ident = ident_columns[:, 0:C]
        column = {n: ident_columns[:, C + k:C + k + 1] for k, n in enumerate(COLUMNS)}
        constants = sb("constants", [C, sum(CONSTANT_WIDTHS)])
        at, views = 0, {}
        for name, width in zip(CONSTANTS, CONSTANT_WIDTHS):
            views[name] = constants[:, at:at + width]
            at += width
        small = sb("small", [CQ, SMALL_WIDTH])
        values = sb("values", [C, 5 * C])
        blocks = sb("blocks", [C, 2, 3, BS])
        layer3 = sb("layer3", [C, 4 * C + 1])

        uw = {n: sb(f"uw{n}", [C, C + 1]) for n in (0, 2, 3)}
        vw = {n: sb(f"vw{n}", [C, CV]) for n in (0, 2, 3)}
        vb = {n: sb(f"vb{n}", [C, CV]) for n in (0, 2, 3)}
        bq3_rows = sb("bq3_rows", [C, C])
        bv3_rows = sb("bv3_rows", [C, C])
        half_sum = sb("half_sum", [C, 2, 2, BS])
        sum_dif = sb("sum_dif", [C, 2, 2, BS])
        diagonal = sb("diagonal", [C, 2, 3, C])
        i_plus_b = sb("i_plus_b", [C, C])
        mixer = sb("mixer", [C, 4, C])
        y_bias = sb("y_bias", [C, 2])
        minus_half = sb("minus_half", [C, 1])
        warm_up = sb("warm_up", [C, TOKENS])
        act_warm = sb("act_warm", [C, 1])
        one = sb("one", [C, 1])

        images = sb("images", [TILE, BATCH, TILES, C])

        staged = sb("staged", [TILE, 2, TILES, C])

        xt = sb("xt", [C, 2, TILES, TILE])
        u = sb("u", [C, 2, TILES, TILE])
        v = sb("v", [TILE, 2, TILES, CV])
        negated = sb("negated", [TILE, 2, TILES, TOKENS])
        lowest = sb("lowest", [TILE, 2, TILES])
        probs = sb("probs", [TILE, 2, TILES, TOKENS])
        total = sb("total", [TILE, 2, TILES])
        inverse = sb("inverse", [TILE, 2, TILES])
        probs_t = sb("probs_t", [TILE, 2, TILES, TOKENS])
        z = sb("z", [C, 2, FREQ])
        of_sums = sb("of_sums", [C, 2, SUMS])
        first = sb("first", [C, 2, FREQ])
        k_act = sb("k_act", [C, 2, FREQ])
        n_act = sb("n_act", [C, 2, FREQ])
        y_top = sb("y_top", [C, 2, TILES, TILE])
        y = sb("y", [C, 2, TILES, TILE])
        g = sb("g", [TILE, 2, TILES, C])
        stats = sb("stats", [C, 2, 2, 3])
        mean_sum = sb("mean_sum", [C, 2])
        deviation = sb("deviation", [C, 2, 2])
        square = sb("square", [C, 2, 2])
        spreads = sb("spreads", [C, 2, 2])
        spread = sb("spread", [C, 2])
        group_var = sb("group_var", [C, 2])
        rstd = sb("rstd", [C, 2])
        gn_scale = sb("gn_scale", [C, 2])
        gn_product = sb("gn_product", [C, 2])
        gn_shift = sb("gn_shift", [C, 2])

        banks = ctx.enter_context(nc.psum_tensor("banks", [128, 8, 512], fp32))

        def xt_bank(half):
            return banks[:, half, :]

        def energy_bank(half):
            return banks[:, 2 + half, :]

        def value_bank(half):
            return banks[:, 4 + half, :]

        def mixed_bank(half):
            return banks[:, 6 + half, :]

        GN = TOKENS
        products = {0: energy_bank(1)[:, 0:C + 3], 2: mixed_bank(0)[:, 0:C + 3],
                    3: mixed_bank(1)[:, 0:C + 3]}
        value_product = mixed_bank(1)[:, C + 3:2 * C + 3]
        bias_product = mixed_bank(1)[:, 2 * C + 3:3 * C + 3]

        ident_loaded = sem("ident_loaded")
        small_loaded = sem("small_loaded")
        values_loaded = sem("values_loaded")
        blocks_loaded = sem("blocks_loaded")
        constants_loaded = sem("constants_loaded")
        layer3_loaded = sem("layer3_loaded")
        x_loaded = [sem(f"x_loaded{k}") for k in range(len(LOADS))]
        stored = sem("stored")
        warm_up_ready = sem("warm_up_ready")
        uw_psum = {n: sem(f"uw_psum{n}") for n in (0, 2, 3)}
        uw_ready = {n: sem(f"uw_ready{n}") for n in (0, 2, 3)}
        vw_ready = {n: sem(f"vw_ready{n}") for n in (0, 2, 3)}
        rows3_ready = sem("rows3_ready")
        halves_made = sem("halves_made")
        diagonal_ready = sem("diagonal_ready")
        mixer_psum = sem("mixer_psum")
        mixer_ready = sem("mixer_ready")
        pool_constants = sem("pool_constants")

        xt_psum = {n: sem(f"xt_psum{n}") for n in (0, 2, 3)}
        xt_ready = {n: sem(f"xt_ready{n}") for n in (0, 2, 3)}
        u_psum = {n: sem(f"u_psum{n}") for n in (0, 2, 3)}
        u_ready = {n: sem(f"u_ready{n}") for n in (0, 2, 3)}
        v_psum = {n: sem(f"v_psum{n}") for n in (0, 2, 3)}
        v_ready = {n: sem(f"v_ready{n}") for n in (0, 2, 3)}
        energy_psum = {n: sem(f"energy_psum{n}") for n in (0, 2, 3)}
        negated_ready = {n: sem(f"negated_ready{n}") for n in (0, 2, 3)}
        probs_ready = {n: sem(f"probs_ready{n}") for n in (0, 2, 3)}
        probs_t_psum = {n: sem(f"probs_t_psum{n}") for n in (0, 2, 3)}
        probs_t_ready = {n: sem(f"probs_t_ready{n}") for n in (0, 2, 3)}
        inverse_ready = {n: sem(f"inverse_ready{n}") for n in (0, 2, 3)}
        mixed_psum = {n: sem(f"mixed_psum{n}") for n in (0, 2, 3)}
        image_staged = {n: sem(f"image_staged{n}") for n in range(LAYERS)}
        layer_done = {n: sem(f"layer_done{n}") for n in range(LAYERS)}

        z_psum, z_ready = sem("z_psum"), sem("z_ready")
        w_psum, of_sums_ready = sem("w_psum"), sem("of_sums_ready")
        first_ready, act_ready = sem("first_ready"), sem("act_ready")
        y_psum, y_top_ready, y_ready = sem("y_psum"), sem("y_top_ready"), sem("y_ready")
        g_psum, g_ready = sem("g_psum"), sem("g_ready")
        back_psum = sem("back_psum")

        stats_ready, mean_sum_ready = sem("stats_ready"), sem("mean_sum_ready")
        group_mean_psum, deviation_ready = sem("group_mean_psum"), sem("deviation_ready")
        square_ready, spread_ready = sem("square_ready"), sem("spread_ready")
        variance_psum, group_var_ready = sem("variance_psum"), sem("group_var_ready")
        rstd_ready, gn_scale_ready = sem("rstd_ready"), sem("gn_scale_ready")
        gn_product_ready, gn_shift_ready = sem("gn_product_ready"), sem("gn_shift_ready")

        weights_parts = 4

        def transposed(n):
            return z_psum if n == MIXER else xt_psum[n]

        def partners(t, half, start, step, length):
            whole = t[:, half, start:start + 1]
            return bass.AP(t, whole.offset, [list(whole.ap[0]), [step, 2], [1, length]])

        def flat(t):
            return t.rearrange("p t k -> p (t k)")

        def halves(columns):
            return columns.rearrange("p (a b) -> p a b", a=2)

        def two_runs(run, distance):
            return bass.AP(run.tensor, run.offset, [[distance * C, 2]] + [list(e) for e in run.ap])

        x_tokens = x.rearrange("b h w c -> b (h w) c")
        out_tokens = out.rearrange("b h w c -> b (h w) c")

        def pieces():
            for tile, runs in enumerate(ROW_RUNS):
                p = 0
                for h, n, d in runs:
                    yield tile, p, h * WIDTH, n * WIDTH, d * WIDTH
                    p += 2 * n * WIDTH

        block = ctx.enter_context(nc.Block())

        def load(engine, k, tiles):
            begin, end = LOADS[k]
            for tile, p, token, n, d in pieces():
                if tile not in tiles:
                    continue
                if end == begin + 1:
                    engine.dma_start(images[p:p + 2 * n, begin, tile, :],
                                     two_runs(x_tokens[begin, token:token + n], d)).then_inc(
                                         x_loaded[k], 16)
                else:
                    for far in range(2):
                        at = token + far * d
                        engine.dma_start(images[p + far * n:p + far * n + n, begin:end, tile, :],
                                         x_tokens[begin:end, at:at + n].rearrange(
                                             "b t c -> t b c")).then_inc(x_loaded[k], 16)

        def store(engine, i, tiles):
            for tile, p, token, n, d in pieces():
                if tile in tiles:
                    engine.dma_start(two_runs(out_tokens[i, token:token + n], d),
                                     images[p:p + 2 * n, i, tile, :]).then_inc(stored, 16)

        @block.sync
        def _(sp):
            sp.dma_start(small[:, :], small_d).then_inc(small_loaded, 16)
            load(sp, 0, range(TILES))
            load(sp, 1, range(TILES))
            load(sp, 2, (0,))
            sp.dma_start(blocks[:, :, :, :], blocks_d).then_inc(blocks_loaded, 16)
            sp.dma_start(constants[:, :], constants_d).then_inc(constants_loaded, 16)
            with sp.Fori(0, BATCH - 1) as i:
                sp.wait_ge(layer_done[NORMED], (i + 1) * TILES)
                store(sp, i, range(TILES))
            sp.wait_ge(layer_done[NORMED], BATCH * TILES - 1)
            store(sp, BATCH - 1, (0,))
            sp.wait_ge(stored, BATCH * DMAS * 16)

        @block.gpsimd
        def _(pool):
            pool.memset(minus_half[:, :], -0.5).then_inc(pool_constants, 1)
            pool.memset(one[:, :], 1.0).then_inc(pool_constants, 1)
            pool.wait_ge(ident_loaded, 16)
            for rows, name in ((bq3_rows, "bq3"), (bv3_rows, "bv3")):
                pool.tensor_copy(rows[:, :], column[name].to_broadcast([C, C])).then_inc(
                    rows3_ready, 1)

            def mixer_matrices():
                pool.wait_ge(blocks_loaded, 16)
                pool.tensor_tensor(sum_dif[:, 0], blocks[:, 0, 1:3], blocks[:, 1, 1:3],
                                   ALU.add).then_inc(halves_made, 1)
                pool.tensor_tensor(sum_dif[:, 1], blocks[:, 0, 1:3], blocks[:, 1, 1:3],
                                   ALU.subtract).then_inc(halves_made, 1)
                pool.wait_ge(halves_made, 2)
                pool.tensor_scalar(half_sum[:, :, :, :], sum_dif[:, :, :, :], 0.5, None,
                                   ALU.mult).then_inc(halves_made, 1)
                pool.wait_ge(halves_made, 3)
                pool.wait_ge(constants_loaded, 16)
                mask = views["mask"].rearrange("p (k o) -> p k o", k=BLOCKS)
                for part in range(2):
                    for which in range(3):
                        source = half_sum[:, part, which - 1] if which else blocks[:, part, 0]
                        pool.tensor_tensor(
                            diagonal[:, part, which].rearrange("p (k o) -> p k o", k=BLOCKS), mask,
                            source.unsqueeze(1).to_broadcast([C, BLOCKS, BS]),
                            ALU.mult).then_inc(diagonal_ready, 1)
                pool.wait_ge(diagonal_ready, 6)
                pool.tensor_tensor(i_plus_b[:, :], diagonal[:, 1, 1], ident,
                                   ALU.add).then_inc(diagonal_ready, 1)

            def stage(job):
                n, i, half = job
                if n > 0:
                    pool.wait_ge(layer_done[n - 1], (i + 1) * TILES)
                if not isinstance(i, int) or i >= 2:
                    pool.wait_ge(transposed(n), i - 1)
                elif n > 0:
                    pool.wait_ge(transposed(n - 1), i - 1 + BATCH)
                pool.tensor_tensor(flat(staged[:, half]), flat(images[:, i]),
                                   one[:, :].to_broadcast([TILE, TILES * C]),
                                   ALU.mult).then_inc(image_staged[n], 1)

            def inverse_deviation(i, half):
                pool.wait_ge(group_var_ready, i + 1)
                pool.tensor_tensor(rstd[:, half:half + 1], group_var[:, half:half + 1],
                                   minus_half[:, :], ALU.pow).then_inc(rstd_ready, 1)

            pool.wait_ge(pool_constants, 2)
            pool.wait_ge(x_loaded[2], 2 * DMAS * 16)
            for n in range(LAYERS):
                if n > 0:
                    stage(Job(n, 0, 0))
                    stage(Job(n, 1, 1))
                with pool.Fori(1, BATCH // 2) as pair:
                    for half in range(2):
                        stage(Job(n, pair * 2 + half, half))
                        if n == NORMED:
                            inverse_deviation(pair * 2 + half - 2, half)
                if n == 0:
                    mixer_matrices()
            for i in range(BATCH - 2, BATCH):
                inverse_deviation(i, i % 2)

        @block.tensor
        def _(pe):
            def small_products(n, wq_t, bk_wk_t, bq, bq_rows):
                b = products[n]
                bk, wk_t = bk_wk_t[:, 0:1], bk_wk_t[:, 1:C + 1]
                nc.tensor.matmul(b[:, 0:C + 1], wq_t, bk_wk_t, start=True, stop=True)
                nc.tensor.matmul(b[:, C + 1:C + 2], wk_t, bq, start=True, stop=True)
                nc.tensor.matmul(b[:, C + 2:C + 3], bq_rows, bk,
                                 start=True, stop=True).then_inc(uw_psum[n], 1)

            def plain_products(n):
                parts = small[:, SMALL_AT[n]:SMALL_AT[n] + SMALL_WIDTH // 2]
                small_products(n, parts[:, 0:C], parts[:, C:2 * C + 1],
                               parts[:, 2 * C + 1:2 * C + 2], parts[:, 2 * C + 1:3 * C + 1])

            def layer3_products():
                pe.wait_ge(layer3_loaded, 16)
                pe.wait_ge(ident_loaded, 16)
                pe.wait_ge(rows3_ready, 2)
                wv_t, wo = layer3[:, 2 * C + 1:3 * C + 1], layer3[:, 3 * C + 1:4 * C + 1]
                nc.tensor.matmul(value_product, wv_t, wo, start=True, stop=True)
                nc.tensor.matmul(bias_product, bv3_rows[:, :], wo, start=True, stop=True)
                small_products(3, layer3[:, 0:C], layer3[:, C:2 * C + 1], column["bq3"],
                               bq3_rows[:, :])

            def mixer_products():
                pe.wait_ge(diagonal_ready, 7)
                b = energy_bank(0)
                cas = views["cas"]
                a2, a2_t, b2_t = diagonal[:, 0, 1], diagonal[:, 0, 2], diagonal[:, 1, 2]
                nc.tensor.matmul(b[:, 0:C], cas, diagonal[:, 0, 0], start=True, stop=True)
                nc.tensor.matmul(b[:, C:2 * C], cas, diagonal[:, 1, 0], start=True, stop=True)
                nc.tensor.matmul(b[:, 2 * C:3 * C], a2_t, i_plus_b[:, :], start=True, stop=True)
                nc.tensor.matmul(b[:, 3 * C:4 * C], b2_t, i_plus_b[:, :], start=True, stop=False)
                nc.tensor.matmul(b[:, 3 * C:4 * C], ident, a2, start=False, stop=True)
                nc.tensor.matmul(xt_bank(1)[:, 0:1], i_plus_b[:, :], column["b2k"],
                                 start=True, stop=True).then_inc(mixer_psum, 1)

            def transpose_x(job):
                n, i, half = job
                if n == 0 and isinstance(i, int) and i < 2:
                    pe.wait_ge(x_loaded[i], DMAS * 16)
                    pe.wait_ge(ident_loaded, 16)
                    source = images[:, i]
                else:
                    pe.wait_ge(image_staged[n], i - 1 if n == 0 else i + 1)
                    source = staged[:, half]
                if n == NORMED:
                    if isinstance(i, int) and i < 2:
                        pe.wait_ge(xt_ready[n - 1], i - 1 + BATCH)
                    else:
                        pe.wait_ge(xt_ready[n], i - 1)
                for tile in range(TILES):
                    mm = nc.tensor.transpose(xt_bank(half)[:, tile * TILE:(tile + 1) * TILE],
                                             source[:, tile, :], ident)
                mm.then_inc(xt_psum[n], 1)

            def project_u(job):
                n, i, half = job
                pe.wait_ge(xt_ready[n], i + 1)
                if isinstance(i, int) and i == 0:
                    pe.wait_ge(uw_ready[n], 1)
                nc.tensor.matmul(energy_bank(half)[:, 0:TOKENS], uw[n][:, 0:C], xt[:, half],
                                 start=True, stop=True).then_inc(u_psum[n], 1)

            def project_v(job):
                n, i, half = job
                if isinstance(i, int) and i == 0:
                    pe.wait_ge(vw_ready[n], weights_parts)
                if isinstance(i, int) and i < 2 and n == MIXER + 1:
                    pe.wait_ge(y_ready, BATCH - 1 + i)
                for tile in range(TILES):
                    mm = nc.tensor.matmul(value_bank(half)[:, tile * CV:(tile + 1) * CV],
                                          xt[:, half, tile, :], vw[n][:, :],
                                          start=True, stop=True)
                mm.then_inc(v_psum[n], 1)

            def energies(job):
                n, i, half = job
                pe.wait_ge(u_ready[n], i + 1)
                for tile in range(TILES):
                    mm = nc.tensor.matmul(
                        energy_bank(half)[:, tile * TOKENS:(tile + 1) * TOKENS],
                        u[:, half, tile, :], xt[:, half], start=True, stop=True)
                mm.then_inc(energy_psum[n], 1)

            def transpose_probs(job):
                n, i, half = job
                for tile in range(TILES):
                    pe.wait_ge(probs_ready[n], i * TILES + tile + 1)
                    for m in range(TILES):
                        at = m * TOKENS + tile * TILE
                        mm = nc.tensor.transpose(value_bank(half)[:, at:at + TILE],
                                                 probs[:, half, tile, m * TILE:(m + 1) * TILE],
                                                 ident)
                mm.then_inc(probs_t_psum[n], 1)

            def mix_values(job):
                n, i, half = job
                pe.wait_ge(probs_t_ready[n], i + 1)
                if n == 0:
                    pe.wait_ge(vw_ready[2], weights_parts)
                    pe.wait_ge(vw_ready[3], weights_parts)
                if n == MIXER + 1:
                    pe.wait_ge(layer_done[MIXER], BATCH * TILES)
                for tile in range(TILES):
                    for m in range(TILES):
                        mm = nc.tensor.matmul(mixed_bank(half)[:, tile * C:(tile + 1) * C],
                                              probs_t[:, half, m, tile * TILE:(tile + 1) * TILE],
                                              v[:, half, m, 0:C],
                                              start=(m == 0), stop=(m == TILES - 1))
                mm.then_inc(mixed_psum[n], 1)

            def forward_tokens(job):
                _, i, half = job
                pe.wait_ge(image_staged[MIXER], i + 1)
                if isinstance(i, int) and i == 1:
                    pe.wait_ge(mixer_ready, 3)
                sums_and_differences = halves(xt_bank(half)[:, 0:FREQ])
                at = 0
                for tile in range(TILES):
                    pairs = HALF[tile]
                    mm = nc.tensor.matmul(sums_and_differences[:, :, at:at + pairs],
                                          staged[:, half, tile, :],
                                          halves(views["forward"][:, 2 * at:2 * (at + pairs)]),
                                          start=True, stop=True)
                    at += pairs
                mm.then_inc(z_psum, 1)

            def first_product(job):
                _, i, half = job
                pe.wait_ge(z_ready, i + 1)
                if isinstance(i, int) and i == 0:
                    pe.wait_ge(mixer_ready, 1)
                b = energy_bank(half)
                nc.tensor.matmul(b[:, 0:SUMS], mixer[:, 0], z[:, half, 0:SUMS],
                                 start=True, stop=True)
                nc.tensor.matmul(b[:, SUMS:FREQ], mixer[:, 1], z[:, half, SUMS:FREQ],
                                 start=True, stop=True).then_inc(w_psum, 1)

            def second_product(job):
                _, i, half = job
                pe.wait_ge(act_ready, i + 1)
                skip = FIXED // 2
                own = [partners(k_act, half, 0, SUMS + skip, TILE // 2),
                       partners(k_act, half, HALF[0], SUMS, TILE // 2)]
                other = [partners(n_act, half, SUMS, skip - SUMS, TILE // 2),
                         partners(n_act, half, SUMS + HALF[0], -SUMS, TILE // 2)]
                for tile in range(TILES):
                    o = halves(value_bank(half)[:, tile * TILE:(tile + 1) * TILE])
                    nc.tensor.matmul(o, mixer[:, 2], own[tile], start=True, stop=False)
                    mm = nc.tensor.matmul(o, mixer[:, 3], other[tile], start=False, stop=True)
                mm.then_inc(y_psum, 1)

            def backward_channels(job):
                _, i, half = job
                pe.wait_ge(y_ready, i + 1)
                for tile in range(TILES):
                    mm = nc.tensor.matmul(mixed_bank(half)[:, tile * C:(tile + 1) * C],
                                          y[:, half, tile, :], views["cas"],
                                          start=True, stop=True)
                mm.then_inc(g_psum, 1)

            def backward_tokens(job):
                _, i, half = job
                pe.wait_ge(g_ready, i + 1)
                for tile in range(TILES):
                    mm = nc.tensor.matmul(mixed_bank(half)[:, tile * C:(tile + 1) * C],
                                          views["backward"][:, tile * TILE:(tile + 1) * TILE],
                                          g[:, half, tile, :], start=True, stop=True)
                mm.then_inc(back_psum, 1)

            def group_means(job):
                _, i, half = job
                pe.wait_ge(mean_sum_ready, i + 1)
                nc.tensor.matmul(xt_bank(half)[:, GN:GN + 1], views["half_average"],
                                 mean_sum[:, half:half + 1],
                                 start=True, stop=True).then_inc(group_mean_psum, 1)

            def group_variances(job):
                _, i, half = job
                pe.wait_ge(spread_ready, i + 1)
                nc.tensor.matmul(xt_bank(half)[:, GN + 1:GN + 2], views["half_average"],
                                 spread[:, half:half + 1],
                                 start=True, stop=True).then_inc(variance_psum, 1)

            def slot(now):
                ahead2, ahead1, this, back1, back2, back3 = (job_at(now, k) for k in range(-2, 4))
                if norms(ahead1):
                    group_means(ahead1)
                if mixes(this):
                    forward_tokens(this)
                elif attends(this) and not norms(this):
                    transpose_x(this)
                if is_job(now, 0, 0):
                    plain_products(2)
                if mixes(back3):
                    backward_channels(back3)
                if mixes(back2):
                    second_product(back2)
                elif attends(back2):
                    transpose_probs(back2)
                if is_job(now, MIXER, 0):
                    mixer_products()
                if attends(back1):
                    energies(back1)
                if norms(ahead2):
                    transpose_x(ahead2)
                if norms(ahead1):
                    group_variances(ahead1)
                if mixes(this):
                    first_product(this)
                if mixes(back3):
                    backward_tokens(back3)
                last_mixed = is_job(now, MIXER + 1, 1)
                if last_mixed:
                    backward_channels(back2)
                if attends(this):
                    project_u(this)
                if attends(back2):
                    mix_values(back2)
                if attends(this):
                    project_v(this)
                if last_mixed:
                    backward_tokens(back2)
                if is_job(now, 0, 1):
                    layer3_products()

            pe.wait_ge(warm_up_ready, 1)
            for _ in range(WARM_UP):
                nc.tensor.matmul(energy_bank(1)[:, 0:TOKENS], warm_up[:, 0:C], warm_up[:, :],
                                 start=True, stop=True)
            pe.wait_ge(small_loaded, 16)
            plain_products(0)
            in_order(pe, slot)

        @block.scalar
        def _(act):
            def move_xt(job):
                n, i, half = job
                act.wait_ge(xt_psum[n], i + 1)
                nc.scalar.activation(flat(xt[:, half]), xt_bank(half)[:, 0:TOKENS],
                                     ACT.Copy).then_inc(xt_ready[n], 1)

            def normalize(job):
                n, i, half = job
                act.wait_ge(gn_scale_ready, i + 1)
                act.wait_ge(gn_shift_ready, i + 1)
                nc.scalar.activation(flat(xt[:, half]), xt_bank(half)[:, 0:TOKENS],
                                     ACT.Identity, bias=gn_shift[:, half:half + 1],
                                     scale=gn_scale[:, half:half + 1]).then_inc(xt_ready[n], 1)

            def move_u(job):
                n, i, half = job
                act.wait_ge(u_psum[n], i + 1)
                nc.scalar.activation(flat(u[:, half]), energy_bank(half)[:, 0:TOKENS],
                                     ACT.Identity, bias=uw[n][:, C:C + 1]).then_inc(
                                         u_ready[n], 1)

            def exponents(job):
                n, i, half = job
                for tile in range(TILES):
                    act.wait_ge(negated_ready[n], i * TILES + tile + 1)
                    nc.scalar.activation(probs[:, half, tile, :], negated[:, half, tile, :],
                                         ACT.Exp, bias=lowest[:, half, tile:tile + 1], scale=-1.0,
                                         accum_out=total[:, half, tile:tile + 1]).then_inc(
                                             probs_ready[n], 1)

            def move_probs(job):
                n, i, half = job
                act.wait_ge(probs_t_psum[n], i + 1)
                nc.scalar.activation(flat(probs_t[:, half]), value_bank(half),
                                     ACT.Copy).then_inc(probs_t_ready[n], 1)

            def move_z(job):
                _, i, half = job
                act.wait_ge(z_psum, i + 1)
                nc.scalar.activation(z[:, half], xt_bank(half)[:, 0:FREQ], ACT.Copy).then_inc(
                    z_ready, 1)

            def move_of_sums(job):
                _, i, half = job
                act.wait_ge(w_psum, i + 1)
                nc.scalar.activation(of_sums[:, half], energy_bank(half)[:, 0:SUMS],
                                     ACT.Copy).then_inc(of_sums_ready, 1)

            def activate(job):
                _, i, half = job
                act.wait_ge(first_ready, i + 1)
                nc.scalar.activation(k_act[:, half], first[:, half], ACT.Relu,
                                     bias=column["b1k"])
                nc.scalar.activation(n_act[:, half], first[:, half], ACT.Relu,
                                     bias=column["b1n"]).then_inc(act_ready, 1)

            def shrink_top(job):
                _, i, half = job
                act.wait_ge(y_psum, i + 1)
                nc.scalar.activation(flat(y_top[:, half]), value_bank(half)[:, 0:TOKENS],
                                     ACT.Relu, bias=y_bias[:, 0:1]).then_inc(y_top_ready, 1)

            def move_g(job):
                _, i, half = job
                act.wait_ge(g_psum, i + 1)
                nc.scalar.activation(flat(g[:, half]), mixed_bank(half)[:, 0:TOKENS],
                                     ACT.Copy).then_inc(g_ready, 1)

            def slot(now):
                this, back1, back2, back3 = (job_at(now, k) for k in range(4))
                if mixes(this):
                    move_z(this)
                if mixes(back3):
                    move_g(back3)
                if norms(this):
                    normalize(this)
                elif attends(this):
                    move_xt(this)
                if mixes(back2):
                    shrink_top(back2)
                elif attends(back2):
                    move_probs(back2)
                if is_job(now, MIXER + 1, 1):
                    move_g(back2)
                if attends(back1):
                    exponents(back1)
                if attends(this):
                    move_u(this)
                if mixes(back1):
                    activate(back1)
                if mixes(this):
                    move_of_sums(this)

            act.dma_start(ident_columns[:, :], ident_columns_d).then_inc(ident_loaded, 16)
            act.wait_ge(warm_up_ready, 1)
            nc.scalar.activation(act_warm[:, :], warm_up[:, 0:1], ACT.Exp)
            act.dma_start(values[:, :], values_d).then_inc(values_loaded, 16)
            act.dma_start(layer3[:, :], layer3_d).then_inc(layer3_loaded, 16)
            load(act, 2, (1,))
            in_order(act, slot)
            act.wait_ge(layer_done[NORMED], BATCH * TILES)
            store(act, BATCH - 1, (1,))

        @block.vector
        def _(dve):
            def attention_weights(n):
                dve.wait_ge(uw_psum[n], 1)
                b = products[n]
                s = SCALE3 if n == 3 else 1.0
                nc.vector.tensor_scalar(uw[n][:, :], b[:, 1:C + 2], -s, None,
                                        ALU.mult).then_inc(uw_ready[n], 1)
                nc.vector.tensor_scalar(vw[n][:, C:CV], b[:, 0:1], s, None,
                                        ALU.mult).then_inc(vw_ready[n], 1)
                nc.vector.tensor_scalar(vb[n][:, C:CV], b[:, C + 2:C + 3], s, None,
                                        ALU.mult).then_inc(vw_ready[n], 1)

            def gated_values(n):
                k = 0 if n == 0 else 1
                gamma = column["gamma0" if n == 0 else "gamma2"]
                nc.vector.tensor_scalar(vw[n][:, 0:C], values[:, k * C:(k + 1) * C], gamma, None,
                                        ALU.mult).then_inc(vw_ready[n], 1)
                nc.vector.tensor_scalar(vb[n][:, 0:C], values[:, (2 + k) * C:(3 + k) * C], gamma,
                                        None, ALU.mult).then_inc(vw_ready[n], 1)

            def output_values():
                nc.vector.tensor_copy(vw[3][:, 0:C], value_product).then_inc(
                    vw_ready[3], 1)
                nc.vector.tensor_tensor(vb[3][:, 0:C], bias_product, values[:, 4 * C:5 * C],
                                        ALU.add).then_inc(vw_ready[3], 1)

            def mixer_weights():
                dve.wait_ge(mixer_psum, 1)
                nc.vector.tensor_copy(mixer[:, :, :].rearrange("p a c -> p (a c)"),
                                      energy_bank(0)).then_inc(mixer_ready, 1)
                for k, sign in ((0, -1.0), (1, 1.0)):
                    nc.vector.tensor_scalar(y_bias[:, k:k + 1], xt_bank(1)[:, 0:1],
                                            column["b2n"], sign * SHRINK, ALU.add,
                                            ALU.add).then_inc(mixer_ready, 1)

            def move_v(job):
                n, i, half = job
                if isinstance(i, int) and i == 0:
                    dve.wait_ge(vw_ready[n], weights_parts)
                dve.wait_ge(v_psum[n], i + 1)
                nc.vector.tensor_tensor(
                    v[:, half],
                    value_bank(half)[:, 0:TILES * CV].rearrange("p (t k) -> p t k", t=TILES),
                    vb[n][:, :].unsqueeze(1).to_broadcast([TILE, TILES, CV]),
                    ALU.add).then_inc(v_ready[n], 1)

            def negate_energies(job, tile):
                n, i, half = job
                if tile == 0:
                    dve.wait_ge(v_ready[n], i + 1)
                    dve.wait_ge(energy_psum[n], i + 1)
                nc.vector.tensor_scalar(
                    negated[:, half, tile, :],
                    energy_bank(half)[:, tile * TOKENS:(tile + 1) * TOKENS],
                    v[:, half, tile, C:CV], FMAX, ALU.subtract, ALU.min,
                    accum_out=lowest[:, half, tile:tile + 1]).then_inc(negated_ready[n], 1)

            def invert_totals(job):
                n, i, half = job
                dve.wait_ge(probs_ready[n], i * TILES + TILES)
                nc.vector.reciprocal(inverse[:, half], total[:, half]).then_inc(
                    inverse_ready[n], 1)

            def add_residual(job):
                n, i, half = job
                dve.wait_ge(inverse_ready[n], i + 1)
                dve.wait_ge(mixed_psum[n], i + 1)
                for tile in range(TILES):
                    nc.vector.scalar_tensor_tensor(
                        images[:, i, tile, :], mixed_bank(half)[:, tile * C:(tile + 1) * C],
                        inverse[:, half, tile:tile + 1], images[:, i, tile, :], ALU.mult,
                        ALU.add).then_inc(layer_done[n], 1)

            def shrink(job):
                _, i, half = job
                dve.wait_ge(y_top_ready, i + 1)
                if isinstance(i, int) and i == 0:
                    dve.wait_ge(mixer_ready, 3)
                nc.vector.scalar_tensor_tensor(
                    flat(y[:, half]), value_bank(half)[:, 0:TOKENS], y_bias[:, 1:2],
                    flat(y_top[:, half]), ALU.add, ALU.min).then_inc(y_ready, 1)

            def partners_results(job):
                _, i, half = job
                dve.wait_ge(of_sums_ready, i + 1)
                of_differences = energy_bank(half)[:, SUMS:FREQ]
                nc.vector.tensor_tensor(first[:, half, 0:SUMS], of_sums[:, half],
                                        of_differences, ALU.add)
                nc.vector.tensor_tensor(first[:, half, SUMS:FREQ], of_sums[:, half],
                                        of_differences, ALU.subtract).then_inc(first_ready, 1)

            def add_image(job):
                n, i, half = job
                dve.wait_ge(back_psum, i + 1)
                nc.vector.tensor_tensor(flat(images[:, i]), mixed_bank(half)[:, 0:TOKENS],
                                        flat(images[:, i]), ALU.add).then_inc(
                                            layer_done[n], TILES)

            def channel_stats(job):
                n, i, half = job
                dve.wait_ge(xt_psum[n], i + 1)
                nc.vector.bn_stats(stats[:, half].rearrange("p e s -> p (e s)"),
                                   xt_bank(half)[:, 0:TOKENS]).then_inc(stats_ready, 1)
                dve.wait_ge(stats_ready, i + 1)
                nc.vector.tensor_tensor(mean_sum[:, half:half + 1], stats[:, half, 0, 1:2],
                                        stats[:, half, 1, 1:2], ALU.add).then_inc(
                                            mean_sum_ready, 1)

            def channel_spread(job):
                _, i, half = job
                dve.wait_ge(group_mean_psum, i + 1)
                nc.vector.tensor_scalar(deviation[:, half], stats[:, half, :, 1],
                                        xt_bank(half)[:, GN:GN + 1], None,
                                        ALU.subtract).then_inc(deviation_ready, 1)
                dve.wait_ge(deviation_ready, i + 1)
                nc.vector.tensor_tensor(square[:, half], deviation[:, half], deviation[:, half],
                                        ALU.mult).then_inc(square_ready, 1)
                dve.wait_ge(square_ready, i + 1)
                nc.vector.scalar_tensor_tensor(spreads[:, half], stats[:, half, :, 2],
                                               2.0 / TOKENS, square[:, half], ALU.mult,
                                               ALU.add, accum_out=spread[:, half:half + 1]
                                               ).then_inc(spread_ready, 1)

            def shifted_variance(job):
                _, i, half = job
                dve.wait_ge(variance_psum, i + 1)
                nc.vector.tensor_scalar(group_var[:, half:half + 1],
                                        xt_bank(half)[:, GN + 1:GN + 2], EPS, None,
                                        ALU.add).then_inc(group_var_ready, 1)

            def norm_scales(job):
                _, i, half = job
                this = slice(half, half + 1)
                dve.wait_ge(rstd_ready, i + 1)
                nc.vector.tensor_scalar(gn_scale[:, this], rstd[:, this], column["gn_gamma"],
                                        None, ALU.mult).then_inc(gn_scale_ready, 1)
                nc.vector.tensor_scalar(gn_product[:, this], rstd[:, this], column["gn_gamma"],
                                        xt_bank(half)[:, GN:GN + 1], ALU.mult,
                                        ALU.mult).then_inc(gn_product_ready, 1)
                dve.wait_ge(gn_product_ready, i + 1)
                nc.vector.tensor_scalar(gn_shift[:, this], gn_product[:, this], -1.0,
                                        column["gn_beta"], ALU.mult, ALU.add).then_inc(
                                            gn_shift_ready, 1)

            def slot(now):
                ahead2, ahead1, this, back1, back2, back3 = (job_at(now, k) for k in range(-2, 4))
                if is_job(now, 0, 1):
                    gated_values(2)
                    attention_weights(2)
                if is_job(now, MIXER, 0):
                    mixer_weights()
                if mixes(back2):
                    shrink(back2)
                if attends(back1):
                    negate_energies(back1, 0)
                if attends(back2):
                    invert_totals(back2)
                if norms(ahead1):
                    shifted_variance(ahead1)
                if attends(back1):
                    negate_energies(back1, 1)
                if norms(ahead2):
                    channel_stats(ahead2)
                if norms(ahead1):
                    norm_scales(ahead1)
                if attends(this):
                    move_v(this)
                if mixes(back3):
                    add_image(back3)
                if norms(ahead2):
                    channel_spread(ahead2)
                if attends(back2):
                    add_residual(back2)
                if mixes(this):
                    partners_results(this)
                if is_job(now, MIXER + 1, 1):
                    add_image(back2)
                if is_job(now, 0, 1):
                    attention_weights(3)
                    output_values()

            nc.vector.memset(warm_up[:, :], 0.0).then_inc(warm_up_ready, 1)
            attention_weights(0)
            dve.wait_ge(values_loaded, 16)
            dve.wait_ge(ident_loaded, 16)
            gated_values(0)
            in_order(dve, slot)


def kernel(**inputs):
    import concourse.bacc as bacc
    from concourse.bass_utils import run_bass_kernel_spmd

    a = {k: np.asarray(t) for k, t in inputs.items()}
    tables = {k: t.astype(np.float32) for k, t in shape_constants().items()}

    def side_by_side(parts):
        return np.ascontiguousarray(np.concatenate(parts, axis=1))

    def small(n):
        bq, bk = a[f"L{n}_conv_bq"], a[f"L{n}_conv_bk"]
        return [a[f"L{n}_conv_Wq"].T, bk[:, None], a[f"L{n}_conv_Wk"].T,
                np.broadcast_to(bq[:, None], (CQ, C))]

    def rows(bias):
        return np.broadcast_to(bias[None, :], (C, C))

    def stacked(w):
        return w.transpose(1, 2, 0, 3).reshape(C, 2, BS)

    w1, w2 = a["L1_conv_w1"], a["L1_conv_w2"]
    b1, b2 = a["L1_conv_b1"].reshape(2, C), a["L1_conv_b2"].reshape(2, C)
    cols = [b1[0], b1[1], b2[0], b2[1], a["L3_conv_gn_gamma"], a["L3_conv_gn_beta"],
            a["L3_conv_bq"], a["L3_conv_bv"],
            np.broadcast_to(a["L0_conv_gamma"], (C,)), np.broadcast_to(a["L2_conv_gamma"], (C,))]
    arrays = {
        "x": np.ascontiguousarray(a["x"]),
        "ident_columns": side_by_side([tables["ident"], np.stack(cols, axis=1)]),
        "constants": side_by_side([tables[n] for n in CONSTANTS]),
        "small": side_by_side(small(0) + small(2)),
        "values": side_by_side([a["L0_conv_Wv"], a["L2_conv_Wv"], rows(a["L0_conv_bv"]),
                                rows(a["L2_conv_bv"]), rows(a["L3_conv_bo"])]),
        "blocks": np.ascontiguousarray(np.stack(
            [stacked(w1), stacked(w2), stacked(w2.transpose(0, 1, 3, 2))], axis=2)),
        "layer3": side_by_side([a["L3_conv_wq"].T, a["L3_conv_bk"][:, None], a["L3_conv_wk"].T,
                                a["L3_conv_wv"].T, a["L3_conv_wo"]]),
    }
    nc = bacc.Bacc("TRN2", target_bir_lowering=False, num_devices=1)
    args = [nc.dram_tensor(f"in_{n}", t.shape, mybir.dt.float32, kind="ExternalInput").ap()
            for n, t in arrays.items()]
    out = nc.dram_tensor("out", (BATCH, HEIGHT, WIDTH, C), mybir.dt.float32,
                         kind="ExternalOutput").ap()
    build(nc, *args, out)
    r = run_bass_kernel_spmd(nc, [{f"in_{n}": t for n, t in arrays.items()}], core_ids=[0])
    return r.results[0]["out"]
```
